# Optimizing a Trainium2 kernel written in Bass

```python
import numpy as np
import jax
import jax.numpy as jnp

def _softmax(x, axis=-1):
    return jax.nn.softmax(x, axis=axis)

def _gelu(x):
    return jax.nn.gelu(x, approximate=True)

def _silu(x):
    return jax.nn.silu(x)

def _sigmoid(x):
    return jax.nn.sigmoid(x)

def _layernorm(x, axis=-1, eps=1e-05):
    m = jnp.mean(x, axis=axis, keepdims=True)
    v = jnp.var(x, axis=axis, keepdims=True)
    return (x - m) / jnp.sqrt(v + eps)

def _scatter_add(tgt, idx, src, axis=0):
    return tgt.at[idx].add(src)

def _segment_sum(src, seg, n):
    return jax.ops.segment_sum(src, seg, n)
kernel_name = 'mk_macaron_d1_jaxref_r8_b98d78'

def setup_inputs(seed: int=0):
    np.random.seed(seed)
    _w = jnp.asarray

    def _L0_attn_setup():
        import jax, jax.numpy as jnp
        import numpy as np
        B, N, D = (2, 256, 128)
        H = 16
        HD = D // H
        NEG = -1e+30
        key = jax.random.key(seed)
        ks = jax.random.split(key, 6)
        s = 0.02
        return {'x': jax.random.normal(ks[0], (B, N, D), dtype=jnp.float32), 'Wq': jax.random.normal(ks[1], (D, D), dtype=jnp.float32) * s, 'Wk': jax.random.normal(ks[2], (D, D), dtype=jnp.float32) * s, 'Wv': jax.random.normal(ks[3], (D, D), dtype=jnp.float32) * s, 'Wo': jax.random.normal(ks[4], (D, D), dtype=jnp.float32) * s, 'Wf': jax.random.normal(ks[5], (D, H), dtype=jnp.float32) * s}
    _L0_attn_in = _L0_attn_setup()

    def _L0_ffn_setup():
        import jax, jax.numpy as jnp
        import numpy as np
        TOP_K = 2
        key = jax.random.key(seed)
        k1, k2, k3 = jax.random.split(key, 3)
        B, S, H, E = (4, 256, 128, 8)
        hidden_states = jax.random.normal(k1, (B, S, H), dtype=jnp.float32)
        Wg = jax.random.normal(k2, (H, E), dtype=jnp.float32) * H ** (-0.5)
        We = jax.random.normal(k3, (E, H, H), dtype=jnp.float32) * H ** (-0.5)
        be = jnp.zeros((E, H), dtype=jnp.float32)
        return {'hidden_states': hidden_states, 'Wg': Wg, 'We': We, 'be': be}
    _L0_ffn_in = _L0_ffn_setup()
    _d = {'L0_attn_x': _L0_attn_in['x'], 'L0_attn_Wq': _L0_attn_in['Wq'], 'L0_attn_Wk': _L0_attn_in['Wk'], 'L0_attn_Wv': _L0_attn_in['Wv'], 'L0_attn_Wo': _L0_attn_in['Wo'], 'L0_attn_Wf': _L0_attn_in['Wf'], 'L0_ffn_Wg': _L0_ffn_in['Wg'], 'L0_ffn_We': _L0_ffn_in['We'], 'L0_ffn_be': _L0_ffn_in['be']}
    _x0 = _d['L0_attn_x']
    _d['L0_attn_x'] = jax.random.normal(jax.random.fold_in(jax.random.key(seed), 1), (16, 256, 128), dtype=_x0.dtype)
    del _x0
    return _d

def reference(L0_attn_x, L0_attn_Wq, L0_attn_Wk, L0_attn_Wv, L0_attn_Wo, L0_attn_Wf, L0_ffn_Wg, L0_ffn_We, L0_ffn_be):

    def _L0_attn_ref(x, Wq, Wk, Wv, Wo, Wf):
        import jax, jax.numpy as jnp
        import numpy as np
        B, N, D = (2, 256, 128)
        H = 16
        HD = D // H
        NEG = -1e+30
        b, n, d = x.shape
        h, hd = (H, HD)
        scale = hd ** (-0.5)
        q = (x @ Wq).reshape(b, n, h, hd).transpose(0, 2, 1, 3)
        k = (x @ Wk).reshape(b, n, h, hd).transpose(0, 2, 1, 3)
        v = (x @ Wv).reshape(b, n, h, hd).transpose(0, 2, 1, 3)
        log_f = jax.nn.log_sigmoid(x @ Wf).transpose(0, 2, 1)
        c = jnp.cumsum(log_f, axis=-1)
        scores = jnp.einsum('bhid,bhjd->bhij', q, k) * scale
        scores = scores + c[..., :, None] - c[..., None, :]
        causal = jnp.tril(jnp.ones((n, n), dtype=bool))
        scores = jnp.where(causal, scores, NEG)
        attn = jax.nn.softmax(scores, axis=-1)
        out = jnp.einsum('bhij,bhjd->bhid', attn, v)
        out = out.transpose(0, 2, 1, 3).reshape(b, n, d)
        return out @ Wo

    def _L0_ffn_ref(hidden_states, Wg, We, be):
        import jax, jax.numpy as jnp
        import numpy as np
        TOP_K = 2
        B, S, H = hidden_states.shape
        T = B * S
        x = hidden_states.reshape(T, H)
        probs = jax.nn.softmax(x @ Wg, axis=-1)
        top_vals, top_idx = jax.lax.top_k(probs, TOP_K)
        gates = top_vals / jnp.sum(top_vals, axis=-1, keepdims=True)
        expert_out = jnp.einsum('th,ehd->etd', x, We) + be[:, None, :]
        tok = jnp.arange(T)[:, None]
        sel = expert_out[top_idx, tok, :]
        out = jnp.sum(gates[..., None] * sel, axis=1)
        return out.reshape(B, S, H)
    x = L0_attn_x
    x = x + 0.5 * _L0_ffn_ref(_layernorm(x, axis=-1), L0_ffn_Wg, L0_ffn_We, L0_ffn_be)
    x = x + _L0_attn_ref(_layernorm(x, axis=-1), L0_attn_Wq, L0_attn_Wk, L0_attn_Wv, L0_attn_Wo, L0_attn_Wf)
    x = x + 0.5 * _L0_ffn_ref(_layernorm(x, axis=-1), L0_ffn_Wg, L0_ffn_We, L0_ffn_be)
    return x

_drawn_inputs = setup_inputs


def setup_inputs(seed=0):
    import zlib

    import numpy as np

    out = dict(_drawn_inputs(seed))
    spreads = {'L0_ffn_be': (0.0, 0.1)}
    factors = {'L0_attn_Wq': 8.0, 'L0_attn_Wk': 8.0, 'L0_attn_Wf': 7.049}
    for name, (base, spread) in spreads.items():
        noise = np.random.default_rng([zlib.crc32(name.encode()), seed]).standard_normal(out[name].shape)
        drawn = base * np.exp(spread * noise) if base else spread * noise
        out[name] = jnp.asarray(drawn.astype(out[name].dtype))
    for name, factor in factors.items():
        out[name] = (out[name] * factor).astype(out[name].dtype)
    return out
```

```python
import concourse.bass as bass
from concourse import mybir
from contextlib import ExitStack

FP32 = mybir.dt.float32
FP32R = mybir.dt.float32r
BF16 = mybir.dt.bfloat16
U32 = mybir.dt.uint32
ALU = mybir.AluOpType
ACT = mybir.ActivationFunctionType
AX = mybir.AxisListType

P = 128
EPS = 1e-5
BANK = 512


def at_least(eng, sem, value):
    if isinstance(value, int) and value <= 0:
        return
    eng.wait_ge(sem, value)


def wait_apart(eng, sem, value, counted):
    eng.wait_ge(sem, value)
    eng.sem_inc(counted, 1)


def run_steps(eng, step, first, last, body, unroll):
    lo, hi = body
    for i in range(first, lo):
        step(i, i)
    with eng.Fori(0, (hi - lo) // unroll) as k:
        for part in range(unroll):
            step(k * unroll + (lo + part), lo + part)
    for i in range(hi, last):
        step(i, i)


def load_constants(nc, sb, w, c):
    with ExitStack() as ctx:
        sem = lambda name: ctx.enter_context(nc.semaphore(name))
        loaded, bias_loaded, filled = sem("weights_loaded"), sem("bias_loaded"), sem("filled")
        zeroed = sem("bias_zeroed")
        split_hi, pool_made = sem("split_hi"), sem("pool_made")
        block = ctx.enter_context(nc.Block())
        E, D = c["E"], P

        @block.sync
        def _(sp):
            sp.dma_start(c["we"][:, :, :], w["We"].rearrange("e h d -> h e d")).then_inc(loaded, 16)
            sp.dma_start(c["wg"][:, :], w["Wg"]).then_inc(loaded, 16)
            for name in ("Wq", "Wk", "Wv", "Wo"):
                sp.dma_start(c[name][:, :], w[name]).then_inc(loaded, 16)
            sp.dma_start(c["Wf"][:, :], w["Wf"]).then_inc(loaded, 16)
            sp.wait_ge(zeroed, 1)
            for part in range(3):
                for q in range(4):
                    row = 32 * part + q * E
                    sp.dma_start(c["bias"][row:row + E, q * D:(q + 1) * D], w["be"]).then_inc(bias_loaded, 16)

        @block.gpsimd
        def _(pool):
            nc.gpsimd.memset(c["ident"][:, :], 0.0).then_inc(filled, 1)
            nc.gpsimd.memset(c["bias"][:, :], 0.0).then_inc(zeroed, 1)
            pool.wait_ge(filled, 1)
            nc.gpsimd.affine_select(out=c["ident"][:, :], in_=c["ident"][:, :], compare_op=ALU.not_equal, fill=1.0,
                                    base=0, pattern=[[-1, P]], channel_multiplier=1).then_inc(filled, 1)
            nc.gpsimd.iota(c["expert_no"][:, :], pattern=[[1, E]], base=0, channel_multiplier=0,
                           allow_small_or_imprecise_dtypes=True).then_inc(pool_made, 1)
            nc.gpsimd.memset(c["minus_half"][:, :], -0.5).then_inc(pool_made, 1)

        @block.scalar
        def _(act):
            act.wait_ge(loaded, 16 * 7)
            nc.scalar.activation(c["we_hi"][:, :], c["we"][:, :, :].rearrange("p e d -> p (e d)"), ACT.Copy).then_inc(split_hi, 1)
            nc.scalar.activation(c["wg_hi"][:, :], c["wg"][:, :], ACT.Copy).then_inc(split_hi, 1)

        @block.vector
        def _(dve):
            dve.wait_ge(split_hi, 2)
            nc.vector.tensor_tensor(c["we_lo"][:, :], c["we"][:, :, :].rearrange("p e d -> p (e d)"),
                                    c["we_hi"][:, :].bitcast(FP32), ALU.subtract)
            nc.vector.tensor_tensor(c["wg_lo"][:, :], c["wg"][:, :], c["wg_hi"][:, :].bitcast(FP32), ALU.subtract)
            dve.wait_ge(bias_loaded, 16 * 12)
            nc.vector.tensor_copy(c["bias_split"][:, :], c["bias"][:, :]).then_inc(split_hi, 1)
            dve.wait_ge(split_hi, 3)
            nc.vector.tensor_tensor(c["bias_split"][64:96, :], c["bias"][64:96, :],
                                    c["bias_split"][64:96, :].bitcast(FP32), ALU.subtract)


def moe_layer(nc, c, banks, x_all, tag, x_dram=None, out_dram=None):
    E, Q, G = c["E"], 4, x_all.shape[1] // 4
    D = P
    with ExitStack() as ctx:
        sb = lambda name, shape, dt: ctx.enter_context(nc.sbuf_tensor(tag + name, shape, dt))
        sem = lambda name: ctx.enter_context(nc.semaphore(tag + name))
        stats = sb("stats", [P, 2, Q, 6], FP32)
        moments = sb("moments", [P, 2, Q, 2], FP32)
        var_eps = sb("var_eps", [P, 2, Q], FP32)
        rstd = sb("rstd", [P, 2, Q], FP32)
        xn = sb("xn", [P, 2, Q, D], FP32)
        xt_hi = sb("xt_hi", [P, 2, Q * P], FP32R)
        xt_lo = sb("xt_lo", [P, 2, Q * P], FP32R)
        best = sb("best", [P, Q, 8], FP32)
        best_no = sb("best_no", [P, Q, 8], U32)
        gap = sb("gap", [P, Q], FP32)
        egap = sb("egap", [P, Q], FP32)
        denom = sb("denom", [P, Q], FP32)
        g1 = sb("g1", [P, Q], FP32)
        g2 = sb("g2", [P, Q], FP32)
        hot1 = sb("hot1", [P, Q, E], FP32)
        hot2 = sb("hot2", [P, Q, E], FP32)
        gates = sb("gates", [P, 2, Q, E], FP32)
        gates3 = sb("gates3", [P, 3, Q * E], FP32R)
        gates_t = sb("gates_t", [3 * Q * E, P], FP32R)
        scaled = sb("scaled", [P, 2, 4, D], FP32)
        pair = sb("pair", [P, 2, 2, D], FP32)
        upper = sb("upper", [P, 2, D], FP32)
        lower = sb("lower", [P, 2, 4, D], FP32)

        y_low = [banks[0], banks[2]]
        y_high = [banks[1], banks[3]]
        xt_bank = banks[4]
        gate_bank = banks[5]
        gates_t_bank = banks[6]
        bias_bank = banks[7]
        logits = gate_bank[:, 0:Q * E].rearrange("p (q e) -> p q e", e=E)

        x_in = sem("x_in")
        stat_done, mom_done, eps_done = sem("stat_done"), sem("mom_done"), sem("eps_done")
        rstd_done, xn_done = sem("rstd_done"), sem("xn_done")
        xt_ready, hi_ready, lo_ready = sem("xt_ready"), sem("hi_ready"), sem("lo_ready")
        logits_ready, chain = sem("logits_ready"), sem("gate_chain")
        no_ready, gap_ready, egap_ready = sem("no_ready"), sem("gap_ready"), sem("egap_ready")
        gates_ready, gates_t_ready, gates_t_copied = sem("gates_ready"), sem("gates_t_ready"), sem("gates_t_copied")
        bias_ready, bias_added = sem("bias_ready"), sem("bias_added")
        y_ready, high_used = sem("y_ready"), sem("high_used")
        low_chain, pair_done, upper_done, upper_used = sem("low_chain"), sem("pair_done"), sem("upper_done"), sem("upper_used")
        stored, waited = sem("stored"), sem("waited")
        CH = 8
        block = ctx.enter_context(nc.Block())

        def steps(eng, step):
            run_steps(eng, step, -2, G, (2, G - 2), 2)

        @block.sync
        def _(sp):
            if x_dram is not None:
                load = lambda g: sp.dma_start(
                    x_all[:, bass.ds(g * Q, Q), :],
                    x_dram[bass.ds(g * (Q * P), Q * P), :].rearrange("(q p) d -> p q d", p=P)).then_inc(x_in, 16)
                load(0)
                with sp.Fori(1, G) as g:
                    sp.wait_ge(x_in, g * 16)
                    load(g)
            if out_dram is not None:
                with sp.Fori(0, G) as g:
                    sp.wait_ge(upper_used, g * Q + Q)
                    sp.dma_start(out_dram[bass.ds(g * (Q * P), Q * P), :].rearrange("(q p) d -> p q d", p=P),
                                 x_all[:, bass.ds(g * Q, Q), :]).then_inc(stored, 16)
                sp.wait_ge(stored, 16 * G)

        @block.gpsimd
        def _(pool):
            def step(i, s):
                b = s % 2
                if 0 <= s:
                    for q in range(Q):
                        t = i * Q + q
                        pool.wait_ge(high_used, t + 1)
                        nc.gpsimd.tensor_tensor(pair[:, q % 2], scaled[:, q % 2, 0:2], scaled[:, q % 2, 2:4],
                                                ALU.add).then_inc(pair_done, 1)
                        pool.wait_ge(pair_done, t + 1)
                        at_least(pool, upper_used, t - 1)
                        nc.gpsimd.tensor_tensor(upper[:, q % 2], pair[:, q % 2, 0], pair[:, q % 2, 1],
                                                ALU.add).then_inc(upper_done, 1)
                if s + 2 < G:
                    pool.wait_ge(eps_done, i + 3)
                    nc.gpsimd.tensor_tensor(rstd[:, b], var_eps[:, b], c["minus_half"][:, 0:Q],
                                            ALU.pow).then_inc(rstd_done, 1)
            steps(pool, step)

        @block.scalar
        def _(act):
            def experts(i, s, q):
                t = i * Q + q
                act.wait_ge(y_ready, t + 1)
                at_least(act, pair_done, t - 1)
                for j in range(4):
                    last = nc.scalar.activation(scaled[:, q % 2, j], y_high[q % 2][:, j * D:(j + 1) * D], ACT.Copy,
                                                scale=gates[:, s % 2, q, 4 + j:5 + j])
                last.then_inc(high_used, 1)

            def step(i, s):
                a, n = (s + 1) % 2, i + 2
                A, B = -1 <= s and s + 1 < G, 0 <= s
                if A:
                    act.wait_ge(xt_ready, n)
                    nc.scalar.activation(xt_hi[:, a], xt_bank[:, :], ACT.Copy).then_inc(hi_ready, 1)
                if B:
                    experts(i, s, 0)
                    experts(i, s, 1)
                if A:
                    act.wait_ge(gap_ready, n)
                    nc.scalar.activation(egap[:, :], gap[:, :], ACT.Exp).then_inc(egap_ready, 1)
                if B:
                    experts(i, s, 2)
                if A:
                    act.wait_ge(gates_t_ready, n)
                    nc.scalar.activation(gates_t[:, :], gates_t_bank[0:3 * Q * E, 0:P], ACT.Copy).then_inc(gates_t_copied, 1)
                if B:
                    experts(i, s, 3)
            steps(act, step)

        @block.vector
        def _(dve):
            def normalise(i, s):
                b, n, g = s % 2, i + 3, i + 2
                if x_dram is not None:
                    dve.wait_ge(x_in, n * 16)
                for q in range(Q):
                    last = nc.vector.bn_stats(stats[:, b, q], x_all[:, bass.ds(g * Q + q, 1), :].rearrange("p a d -> p (a d)"))
                last.then_inc(stat_done, 1)
                wait_apart(dve, stat_done, n, waited)
                for q in range(Q):
                    last = nc.vector.bn_aggr(moments[:, b, q], stats[:, b, q])
                last.then_inc(mom_done, 1)
                dve.wait_ge(mom_done, n)
                nc.vector.tensor_scalar(var_eps[:, b], moments[:, b, :, 1], EPS, None, ALU.add).then_inc(eps_done, 1)

            def normalise2(i, s):
                b, n, g = s % 2, i + 3, i + 2
                dve.wait_ge(rstd_done, n)
                for q in range(Q):
                    last = nc.vector.tensor_scalar(xn[:, b, q], x_all[:, bass.ds(g * Q + q, 1), :].rearrange("p a d -> p (a d)"),
                                                   moments[:, b, q, 0:1], rstd[:, b, q:q + 1], ALU.subtract, ALU.mult)
                last.then_inc(xn_done, 1)

            def low_part(i, s):
                a, n = (s + 1) % 2, i + 2
                dve.wait_ge(hi_ready, n)
                nc.vector.tensor_tensor(xt_lo[:, a], xt_bank[:, :], xt_hi[:, a].bitcast(FP32), ALU.subtract).then_inc(lo_ready, 1)

            def link(n, k, ins):
                ins.then_inc(chain, 1)
                dve.wait_ge(chain, (n - 1) * CH + k)

            def pick(i, s):
                n = i + 2
                wait_apart(dve, logits_ready, n, waited)
                for q in range(Q):
                    last = nc.vector.max(best[:, q], logits[:, q])
                link(n, 1, last)
                nc.vector.tensor_tensor(gap[:, :], best[:, :, 1], best[:, :, 0], ALU.subtract).then_inc(gap_ready, 1)
                for q in range(Q):
                    last = nc.vector.max_index(best_no[:, q], best[:, q], logits[:, q])
                last.then_inc(no_ready, 1)
                every = c["expert_no"][:, :].unsqueeze(1).broadcast_to([P, Q, E])
                dve.wait_ge(no_ready, n)
                nc.vector.tensor_tensor(hot1[:, :, :], every, best_no[:, :, 0:1].broadcast_to([P, Q, E]), ALU.is_equal)
                link(n, 2, nc.vector.tensor_tensor(hot2[:, :, :], every, best_no[:, :, 1:2].broadcast_to([P, Q, E]), ALU.is_equal))

            def weigh(i, s):
                a, n = (s + 1) % 2, i + 2
                dve.wait_ge(egap_ready, n)
                link(n, 3, nc.vector.tensor_scalar(denom[:, :], egap[:, :], 2.0, 2.0, ALU.mult, ALU.add))
                link(n, 4, nc.vector.reciprocal(g1[:, :], denom[:, :]))
                nc.vector.tensor_tensor(hot1[:, :, :], hot1[:, :, :], g1[:, :].unsqueeze(2).broadcast_to([P, Q, E]), ALU.mult)
                link(n, 5, nc.vector.tensor_tensor(g2[:, :], egap[:, :], g1[:, :], ALU.mult))
                link(n, 6, nc.vector.tensor_tensor(hot2[:, :, :], hot2[:, :, :], g2[:, :].unsqueeze(2).broadcast_to([P, Q, E]), ALU.mult))
                link(n, 7, nc.vector.tensor_tensor(gates[:, a], hot1[:, :, :], hot2[:, :, :], ALU.add))
                flat = gates[:, a].rearrange("p q e -> p (q e)")
                nc.vector.tensor_copy(gates3[:, 0], flat)
                link(n, 8, nc.vector.tensor_copy(gates3[:, 2], flat))
                nc.vector.tensor_tensor(gates3[:, 1], flat, gates3[:, 0].bitcast(FP32), ALU.subtract).then_inc(gates_ready, 1)

            def experts(i, s, q):
                t = i * Q + q
                x_t = x_all[:, bass.ds(t, 1), :].rearrange("p a d -> p (a d)")
                dve.wait_ge(y_ready, t + 1)
                before = x_t
                for j in range(4):
                    ins = nc.vector.scalar_tensor_tensor(out=lower[:, q % 2, j], in0=y_low[q % 2][:, j * D:(j + 1) * D],
                                                         scalar=gates[:, s % 2, q, j:j + 1], in1=before,
                                                         op0=ALU.mult, op1=ALU.add)
                    before = lower[:, q % 2, j]
                    ins.then_inc(low_chain, 1)
                    dve.wait_ge(low_chain, t * 4 + (j + 1))
                dve.wait_ge(upper_done, t + 1)
                nc.vector.tensor_tensor(x_t, before, upper[:, q % 2], ALU.add).then_inc(upper_used, 1)

            def step(i, s):
                A, B = -1 <= s and s + 1 < G, 0 <= s
                if B:
                    dve.wait_ge(bias_ready, i + 1)
                    xg = x_all[:, bass.ds(i * Q, Q), :].rearrange("p q d -> p (q d)")
                    nc.vector.tensor_tensor(xg, xg, bias_bank[:, :], ALU.add).then_inc(bias_added, 1)
                    dve.wait_ge(bias_added, i + 1)
                if A:
                    low_part(i, s)
                if B:
                    experts(i, s, 0)
                if A:
                    pick(i, s)
                if B:
                    experts(i, s, 1)
                if A:
                    weigh(i, s)
                if B:
                    experts(i, s, 2)
                if s + 2 < G:
                    normalise(i, s)
                if B:
                    experts(i, s, 3)
                if s + 2 < G:
                    normalise2(i, s)
            steps(dve, step)

        @block.tensor
        def _(pe):
            def experts(i, s, q):
                t = i * Q + q
                b = s % 2
                at_least(pe, low_chain, (t - 1) * 4)
                at_least(pe, high_used, t - 1)
                hi, lo = xt_hi[:, b, q * P:(q + 1) * P], xt_lo[:, b, q * P:(q + 1) * P]
                H = 4 * D
                for k, (x_part, w_part) in enumerate(((hi, c["we_hi"]), (hi, c["we_lo"]), (lo, c["we_hi"]))):
                    nc.tensor.matmul(y_low[q % 2][:, :], x_part, w_part[:, 0:H], start=k == 0, stop=k == 2)
                    last = nc.tensor.matmul(y_high[q % 2][:, :], x_part, w_part[:, H:2 * H], start=k == 0, stop=k == 2)
                last.then_inc(y_ready, 1)

            def step(i, s):
                a, n = (s + 1) % 2, i + 2
                A, B = -1 <= s and s + 1 < G, 0 <= s
                if A:
                    pe.wait_ge(xn_done, n)
                    at_least(pe, lo_ready, n - 1)
                    for q in range(Q):
                        last = nc.tensor.transpose(xt_bank[:, q * P:(q + 1) * P], xn[:, a, q], c["ident"][:, :])
                    last.then_inc(xt_ready, 1)
                if B:
                    experts(i, s, 0)
                if A:
                    pe.wait_ge(lo_ready, n)
                    for q in range(Q):
                        hi, lo = xt_hi[:, a, q * P:(q + 1) * P], xt_lo[:, a, q * P:(q + 1) * P]
                        nc.tensor.matmul(logits[:, q], hi, c["wg_hi"][:, :], start=True, stop=False)
                        nc.tensor.matmul(logits[:, q], hi, c["wg_lo"][:, :], start=False, stop=False)
                        last = nc.tensor.matmul(logits[:, q], lo, c["wg_hi"][:, :], start=False, stop=True)
                    last.then_inc(logits_ready, 1)
                if B:
                    experts(i, s, 1)
                    experts(i, s, 2)
                if A:
                    pe.wait_ge(gates_ready, n)
                    nc.tensor.transpose(gates_t_bank[0:3 * Q * E, 0:P], gates3[:, :, :].rearrange("p k n -> p (k n)").bitcast(FP32),
                                        c["ident"][:, :]).then_inc(gates_t_ready, 1)
                if B:
                    experts(i, s, 3)
                if A:
                    pe.wait_ge(gates_t_copied, n)
                    at_least(pe, bias_added, n - 1)
                    nc.tensor.matmul(bias_bank[:, :], gates_t[:, :], c["bias_split"][:, :],
                                     start=True, stop=True).then_inc(bias_ready, 1)
            steps(pe, step)


def attention_layer(nc, c, banks, x_all, S_LEN):
    H, D = c["H"], P
    NSEQ = x_all.shape[1] // 2
    HD = D // H
    NG, NU = 4, H // 4
    ROWS = 3 * HD + 2
    KR = NG * ROWS
    KM = KR + H
    VC = HD + 1
    SCALE = float(HD) ** -0.5
    N = S_LEN
    with ExitStack() as ctx:
        sb = lambda name, shape, dt: ctx.enter_context(nc.sbuf_tensor("a_" + name, shape, dt))
        sem = lambda name: ctx.enter_context(nc.semaphore("a_" + name))
        stats = sb("stats", [P, 2, 6], FP32)
        moments = sb("moments", [P, 2, 2], FP32)
        var_eps = sb("var_eps", [P, 2], FP32)
        rstd = sb("rstd", [P, 2], FP32)
        xn = sb("xn", [P, 2, D], FP32)
        xt = sb("xt", [P, N], FP32)
        f = sb("f", [H, N], FP32)
        neg_abs = sb("neg_abs", [H, N], FP32)
        exp_f = sb("exp_f", [H, N], FP32)
        log_f = sb("log_f", [H, N], FP32)
        log_sig = sb("log_sig", [H, N], FP32)
        neg_c = sb("neg_c", [H, N], FP32)
        c_parts = sb("c_parts", [H, 2, N], FP32R)
        own_u = sb("own_u", [H, NU, N], FP32R)
        wq_gdu = sb("wq_gdu", [P, D], FP32)
        wk_gdu = sb("wk_gdu", [P, D], FP32)
        ones_row = sb("ones_row", [H, N], FP32)
        zero_row = sb("zero_row", [H, N], FP32)
        ones_r = sb("ones_r", [2, NU * N], FP32R)
        q_parts = sb("q_parts", [P, 2, N], FP32R)
        k_parts = sb("k_parts", [P, 2, N], FP32R)
        q_rows = [sb(f"q_rows{b}", [KM, H, N], FP32R) for b in range(3)]
        k_rows = [sb(f"k_rows{b}", [KM, NU, N], FP32R) for b in range(3)]
        v_sb = [sb(f"v{b}", [P, 2, H, VC], FP32) for b in range(3)]
        neg_max = sb("neg_max", [P, 2, H], FP32)
        max_t = [sb(f"max_t{t}", [H, P], FP32R) for t in range(2)]
        weights = [sb(f"weights{n}", [P, 8, P], FP32) for n in range(3)]
        recip = sb("recip", [P, 2 * H], FP32)
        attn = sb("attn", [P, 2 * H, HD], FP32)
        attn_t = sb("attn_t", [P, N], FP32)
        ident16 = sb("ident16", [P, P], BF16)
        mask16 = sb("mask16", [P, 4, P], BF16)
        mask16_t = sb("mask16_t", [P, 4, P], BF16)

        score_bank = banks[0:2]
        wt_bank = [(banks[2], banks[3]), (banks[4], banks[5])]
        out_bank = banks[6]
        side_bank = banks[7]
        out_view = out_bank[:, 0:2 * H * VC].rearrange("p (n v) -> p n v", v=VC)
        q_ps, k_ps = side_bank[:, 0:N], side_bank[:, N:2 * N]

        set_up, zeroed, ones_in = sem("set_up"), sem("zeroed"), sem("ones_in")
        stat_done, mom_done, eps_done = sem("stat_done"), sem("mom_done"), sem("eps_done")
        rstd_done, xn_done = sem("rstd_done"), sem("xn_done")
        xt_ready, xt_copied = sem("xt_ready"), sem("xt_copied")
        f_ready, f_copied, neg_abs_done = sem("f_ready"), sem("f_copied"), sem("neg_abs_done")
        exp_done, log_done, log_sig_done = sem("exp_done"), sem("log_done"), sem("log_sig_done")
        c_done, c_hi_done, c_lo_done = sem("c_done"), sem("c_hi_done"), sem("c_lo_done")
        qk_ready, qk_hi_done, qk_lo_done = sem("qk_ready"), sem("qk_hi_done"), sem("qk_lo_done")
        v_ready, v_copied = sem("v_ready"), sem("v_copied")
        rows_in = sem("rows_in")
        scores_ready, max_done = sem("scores_ready"), sem("max_done")
        max_t_ready, max_t_copied = sem("max_t_ready"), sem("max_t_copied")
        max_in = [sem("max_in0"), sem("max_in1")]
        wt_ready, wt_exp, av_done = sem("wt_ready"), sem("wt_exp"), sem("av_done")
        recip_done, attn_done = sem("recip_done"), sem("attn_done")
        attn_t_ready, attn_t_copied = sem("attn_t_ready"), sem("attn_t_copied")
        proj_ready, proj_added = sem("proj_ready"), sem("proj_added")
        dve_waited = sem("dve_waited")
        k_stored, q_stored, w_ordered = sem("k_stored"), sem("q_stored"), sem("w_ordered")
        LOADS = NG + 1
        raw = lambda tile: tile[(slice(None),) * len(tile.shape)].bitcast(FP32)
        q_dram = nc.dram_tensor("q_stage", (NG, 3 * HD, NU, N), FP32, kind="Internal").ap()
        k_dram = nc.dram_tensor("k_stage", (NG, ROWS, NU, N), FP32, kind="Internal").ap()
        block = ctx.enter_context(nc.Block())

        def steps(eng, step):
            run_steps(eng, step, -2, NSEQ + 2, (2, 2 + (NSEQ - 4) // 3 * 3), 3)

        @block.sync
        def _(sp):
            sp.wait_ge(zeroed, 1)
            ones = ones_r[:, :].bitcast(FP32).rearrange("r (u n) -> r u n", u=NU)
            for b in range(3):
                for g in range(NG):
                    sp.dma_start(raw(q_rows[b])[ROWS * g + 3 * HD:ROWS * (g + 1), NU * g:NU * (g + 1), :], ones).then_inc(ones_in, 16)
            sp.wait_ge(set_up, 2 + NG)
            for b in range(3):
                sp.dma_start(raw(k_rows[b])[KR:KM, :, :], raw(own_u)).then_inc(ones_in, 16)

            def max_rows(i, s, t):
                sp.wait_ge(max_t_copied, i * 2 + t + 1)
                for g in range(NG):
                    sp.dma_start(raw(q_rows[s % 3])[KR + NU * g:KR + NU * (g + 1), NU * g:NU * (g + 1), t * P:(t + 1) * P],
                                 raw(max_t[t])[NU * g:NU * (g + 1), :].unsqueeze(1).broadcast_to([NU, NU, P])).then_inc(max_in[t], 16)

            def step(i, s):
                F = 0 <= s + 1 < NSEQ
                b, n = (s + 1) % 3, i + 2
                if 0 <= s - 1 < NSEQ:
                    max_rows(i - 1, s - 1, 1)
                if F:
                    at_least(sp, rows_in, (n - 1) * 16 * LOADS)
                    sp.wait_ge(qk_lo_done, n * 2)
                    for r, part in enumerate((0, 1, 0)):
                        sp.dma_start(k_dram[:, r * HD:(r + 1) * HD].rearrange("g d u n -> g (d u) n"),
                                     raw(k_parts)[:, part, :]).then_inc(k_stored, 16)
                    for r, part in enumerate((0, 0, 1)):
                        sp.dma_start(q_dram[:, r * HD:(r + 1) * HD].rearrange("g d u n -> g (d u) n"),
                                     raw(q_parts)[:, part, :]).then_inc(q_stored, 16)
                if 0 <= s < NSEQ:
                    max_rows(i, s, 0)
                if F:
                    sp.wait_ge(c_lo_done, n)
                    for part in range(2):
                        sp.dma_start(k_dram[:, 3 * HD + part], raw(c_parts)[:, part, :]).then_inc(k_stored, 16)
                    at_least(sp, wt_ready, (i - 1) * 6)
                    sp.wait_ge(q_stored, n * 16 * 3)
                    for g in range(NG):
                        sp.dma_start(raw(q_rows[b])[ROWS * g:ROWS * g + 3 * HD, NU * g:NU * (g + 1), :],
                                     q_dram[g]).then_inc(rows_in, 16)
                    sp.wait_ge(k_stored, n * 16 * 5)
                    sp.dma_start(raw(k_rows[b])[0:KR, :, :], k_dram.rearrange("g r u n -> (g r) u n")).then_inc(rows_in, 16)
            steps(sp, step)

        @block.gpsimd
        def _(pool):
            for b in range(3):
                last = nc.gpsimd.memset(q_rows[b][:, :, :].bitcast(U32), 0)
            nc.gpsimd.memset(ones_r[:, :].bitcast(FP32), 1.0).then_inc(zeroed, 1)
            for b in range(3):
                nc.gpsimd.memset(v_sb[b][:, :, :, HD:VC], 1.0)
            nc.gpsimd.memset(ones_row[:, :], 1.0)
            nc.gpsimd.memset(zero_row[:, :], 0.0)
            nc.gpsimd.memset(raw(own_u).bitcast(U32), 0)
            nc.gpsimd.memset(ident16[:, :], 0.0)
            nc.gpsimd.memset(mask16_t[:, :, :], 0.0)
            nc.gpsimd.memset(mask16[:, :, :], 0.0).then_inc(set_up, 1)
            pool.wait_ge(set_up, 1)
            nc.gpsimd.affine_select(out=ident16[:, :], in_=ident16[:, :], compare_op=ALU.not_equal, fill=1.0,
                                    base=0, pattern=[[-1, P]], channel_multiplier=1)
            nc.gpsimd.affine_select(out=mask16_t[:, :, :], in_=mask16_t[:, :, :], compare_op=ALU.is_ge, fill=-1e30,
                                    base=0, pattern=[[0, 4], [1, P]], channel_multiplier=-1)
            nc.gpsimd.affine_select(out=mask16[:, :, :], in_=mask16[:, :, :], compare_op=ALU.is_ge, fill=-1e30,
                                    base=0, pattern=[[0, 4], [-1, P]], channel_multiplier=1).then_inc(set_up, 1)
            for g in range(NG):
                pool.wait_ge(set_up, 2 + g)
                nc.gpsimd.affine_select(out=own_u[:, :, :], in_=raw(own_u), compare_op=ALU.not_equal, fill=1.0,
                                        base=-NU * g, pattern=[[-1, NU], [0, N]], channel_multiplier=1).then_inc(set_up, 1)

            def step(i, s):
                for j in range(6):
                    if j == 4 and 0 <= s + 1 < NSEQ:
                        n = i + 2
                        pool.wait_ge(c_done, n)
                        at_least(pool, rows_in, (n - 1) * 16 * LOADS)
                        nc.gpsimd.tensor_tensor(c_parts[:, 0], neg_c[:, :], zero_row[:, :], ALU.add).then_inc(c_hi_done, 1)
                        pool.wait_ge(c_hi_done, n)
                        nc.gpsimd.tensor_tensor(c_parts[:, 1], neg_c[:, :], c_parts[:, 0].bitcast(FP32), ALU.subtract).then_inc(c_lo_done, 1)
                    if j == 5 and 0 <= s + 2 < NSEQ:
                        pool.wait_ge(eps_done, i + 3)
                        nc.gpsimd.tensor_tensor(rstd[:, :], var_eps[:, :], c["minus_half"][:, 0:2], ALU.pow).then_inc(rstd_done, 1)
            steps(pool, step)

        @block.scalar
        def _(act):
            def copy_max(i, s, t):
                act.wait_ge(max_t_ready, i * 2 + t + 1)
                at_least(act, max_in[t], i * 16 * NG)
                nc.scalar.activation(max_t[t][:, :], side_bank[0:H, 0:P], ACT.Copy).then_inc(max_t_copied, 1)

            def exp(i, s, k):
                act.wait_ge(wt_ready, i * 6 + k + 1)
                at_least(act, av_done, i * 6 + k - 2)
                lo, hi = wt_bank[k % 2]
                for part, bank in enumerate((lo, hi)):
                    last = nc.scalar.activation(weights[k % 3][:, 4 * part:4 * part + 4, :].rearrange("p h n -> p (h n)"),
                                                bank[:, :], ACT.Exp)
                last.then_inc(wt_exp, 1)

            for made, name in ((wq_gdu, "Wq"), (wk_gdu, "Wk")):
                nc.scalar.activation(made[:, :].rearrange("p (g d u) -> p g d u", g=NG, u=NU),
                                     c[name][:, :].rearrange("p (g u d) -> p g d u", g=NG, u=NU), ACT.Copy).then_inc(w_ordered, 1)

            def step(i, s):
                X, F, T = 0 <= s - 1 < NSEQ, 0 <= s + 1 < NSEQ, 0 <= s - 2 < NSEQ
                n = i + 2
                for j in range(6):
                    if j == 0 and X:
                        copy_max(i - 1, s - 1, 1)
                    if j == 3 and 0 <= s < NSEQ:
                        copy_max(i, s, 0)
                    if X:
                        exp(i - 1, s - 1, j)
                    if j == 0 and F:
                        act.wait_ge(xt_ready, n)
                        nc.scalar.activation(xt[:, :], side_bank[:, 0:N], ACT.Copy).then_inc(xt_copied, 1)
                    if j == 1 and F:
                        act.wait_ge(f_ready, n)
                        nc.scalar.activation(f[:, :], side_bank[0:H, 0:N], ACT.Copy).then_inc(f_copied, 1)
                    if j == 2 and F:
                        act.wait_ge(qk_ready, n)
                        at_least(act, rows_in, (n - 1) * 16 * LOADS)
                        nc.scalar.activation(q_parts[:, 0, :], q_ps, ACT.Copy, scale=SCALE)
                        nc.scalar.activation(k_parts[:, 0, :], k_ps, ACT.Copy).then_inc(qk_hi_done, 1)
                    if j == 2 and F:
                        act.wait_ge(neg_abs_done, n)
                        nc.scalar.activation(exp_f[:, :], neg_abs[:, :], ACT.Exp).then_inc(exp_done, 1)
                        act.wait_ge(exp_done, n)
                        nc.scalar.activation(log_f[:, :], exp_f[:, :], ACT.Ln, bias=1.0).then_inc(log_done, 1)
                    if j == 4 and F:
                        act.wait_ge(v_ready, n)
                        nc.scalar.activation(v_sb[(s + 1) % 3][:, :, :, 0:HD].rearrange("p t h d -> p (t h) d"),
                                             side_bank[:, 0:2 * D].rearrange("p (n d) -> p n d", d=HD), ACT.Copy).then_inc(v_copied, 1)
                    if j == 4 and T:
                        act.wait_ge(attn_t_ready, i - 1)
                        nc.scalar.activation(attn_t[:, :], side_bank[:, 0:N], ACT.Copy).then_inc(attn_t_copied, 1)
            steps(act, step)

        @block.vector
        def _(dve):
            def tile(t):
                return x_all[:, bass.ds(t, 1), :].rearrange("p a d -> p (a d)")

            def row_max(i, s, p):
                dve.wait_ge(scores_ready, i * 12 + p + 1)
                t, first, heads = (0, 4 * p, 4) if p < 4 else (1, 2 * (p - 4), 2)
                nc.vector.tensor_reduce(neg_max[:, t, first:first + heads],
                                        score_bank[p % 2][:, :].rearrange("p (h n) -> p h n", h=heads),
                                        AX.X, ALU.max, negate=True).then_inc(max_done, 1)

            def step(i, s):
                S, F, T, A0 = 0 <= s < NSEQ, 0 <= s + 1 < NSEQ, 0 <= s - 2 < NSEQ, 0 <= s + 2 < NSEQ
                n = i + 2
                for j in range(6):
                    if S:
                        row_max(i, s, 2 * j)
                        row_max(i, s, 2 * j + 1)
                    if j == 1 and T:
                        dve.wait_ge(av_done, (i - 1) * 6)
                        nc.vector.reciprocal(recip[:, :], out_view[:, :, HD]).then_inc(recip_done, 1)
                        dve.wait_ge(recip_done, i - 1)
                        nc.vector.tensor_tensor(attn[:, :, :], out_view[:, :, 0:HD],
                                                recip[:, :].unsqueeze(2).broadcast_to([P, 2 * H, HD]), ALU.mult).then_inc(attn_done, 1)
                    if j == 1 and F:
                        dve.wait_ge(f_copied, n)
                        nc.vector.scalar_tensor_tensor(out=neg_abs[:, :], in0=f[:, :], scalar=-1.0, in1=f[:, :],
                                                       op0=ALU.mult, op1=ALU.min).then_inc(neg_abs_done, 1)
                    if j == 2 and F:
                        dve.wait_ge(qk_hi_done, n)
                        nc.vector.scalar_tensor_tensor(out=q_parts[:, 1, :], in0=q_ps, scalar=SCALE,
                                                       in1=q_parts[:, 0, :].bitcast(FP32), op0=ALU.mult, op1=ALU.subtract).then_inc(qk_lo_done, 1)
                        nc.vector.tensor_tensor(k_parts[:, 1, :], k_ps, k_parts[:, 0, :].bitcast(FP32),
                                                ALU.subtract).then_inc(qk_lo_done, 1)
                    if j == 3 and F:
                        dve.wait_ge(log_done, n)
                        nc.vector.scalar_tensor_tensor(out=log_sig[:, :], in0=f[:, :], scalar=0.0, in1=log_f[:, :],
                                                       op0=ALU.min, op1=ALU.subtract).then_inc(log_sig_done, 1)
                        dve.wait_ge(log_sig_done, n)
                        at_least(dve, c_lo_done, n - 1)
                        nc.vector.tensor_tensor_scan(neg_c[:, :], ones_row[:, :], log_sig[:, :], 0.0,
                                                     ALU.mult, ALU.subtract).then_inc(c_done, 1)
                    if j == 4 and A0:
                        for t in range(2):
                            last = nc.vector.bn_stats(stats[:, t], tile((i + 2) * 2 + t))
                        last.then_inc(stat_done, 1)
                        wait_apart(dve, stat_done, i + 3, dve_waited)
                        for t in range(2):
                            last = nc.vector.bn_aggr(moments[:, t], stats[:, t])
                        last.then_inc(mom_done, 1)
                        dve.wait_ge(mom_done, i + 3)
                        nc.vector.tensor_scalar(var_eps[:, :], moments[:, :, 1], EPS, None, ALU.add).then_inc(eps_done, 1)
                    if j == 5 and T:
                        dve.wait_ge(proj_ready, i - 1)
                        pair = x_all[:, bass.ds((i - 2) * 2, 2), :].rearrange("p t d -> p (t d)")
                        nc.vector.tensor_tensor(pair, pair, side_bank[:, 0:2 * D], ALU.add).then_inc(proj_added, 1)
                    if j == 5 and A0:
                        dve.wait_ge(rstd_done, i + 3)
                        for t in range(2):
                            last = nc.vector.tensor_scalar(xn[:, t], tile((i + 2) * 2 + t), moments[:, t, 0:1], rstd[:, t:t + 1],
                                                           ALU.subtract, ALU.mult)
                        last.then_inc(xn_done, 1)
            steps(dve, step)

        @block.tensor
        def _(pe):
            pe.wait_ge(set_up, 2)
            pe.wait_ge(w_ordered, 2)
            pe.wait_ge(ones_in, 16 * 3 * (NG + 1))

            def scores(i, s, p):
                at_least(pe, max_done, i * 12 + p - 1)
                b, bank = s % 3, score_bank[p % 2]
                t, first, heads = (0, 4 * p, 4) if p < 4 else (1, 2 * (p - 4), 2)
                keys = (t + 1) * P
                for n in range(heads):
                    h = first + n
                    nc.tensor.matmul(bank[:, n * keys:(n + 1) * keys], q_rows[b][0:KR, h, t * P:(t + 1) * P],
                                     k_rows[b][0:KR, h % NU, 0:keys], start=n == 0, stop=False, skip_group_check=True)
                own = bank[:, :].rearrange("p (h n) -> p h n", h=heads)[:, :, keys - P:keys]
                nc.tensor.matmul(own, ident16[:, :], mask16[:, 0:heads, :], start=False, stop=True,
                                 skip_group_check=True).then_inc(scores_ready, 1)

            def turned_scores(i, s, k):
                if k == 0:
                    pe.wait_ge(max_in[0], (i + 1) * 16 * NG)
                if k == 2:
                    pe.wait_ge(max_in[1], (i + 1) * 16 * NG)
                at_least(pe, wt_exp, i * 6 + k - 1)
                b = s % 3
                for n, bank in enumerate(wt_bank[k % 2]):
                    t, u, jt = (0, 2 * k + n, 0) if k < 2 else (1, k - 2, n)
                    diagonal = jt == t
                    last = nc.tensor.matmul(bank[:, :], k_rows[b][0:KM, u, jt * P:(jt + 1) * P],
                                            q_rows[b][0:KM, u:H:NU, t * P:(t + 1) * P], start=True, stop=not diagonal)
                    if diagonal:
                        last = nc.tensor.matmul(bank[:, :], ident16[:, :], mask16_t[:, :, :], start=False, stop=True)
                last.then_inc(wt_ready, 1)

            def times_v(i, s, k):
                pe.wait_ge(wt_exp, i * 6 + k + 1)
                if k == 0:
                    at_least(pe, attn_done, i)
                b, w = s % 3, weights[k % 3]
                for n in range(8 if k < 2 else 4):
                    if k < 2:
                        h = NU * (n % 4) + 2 * k + n // 4
                        last = nc.tensor.matmul(out_view[:, h], w[:, n, :], v_sb[b][:, 0, h, :], start=True, stop=True)
                    else:
                        h = NU * n + k - 2
                        nc.tensor.matmul(out_view[:, H + h], w[:, n, :], v_sb[b][:, 0, h, :], start=True, stop=False)
                        last = nc.tensor.matmul(out_view[:, H + h], w[:, 4 + n, :], v_sb[b][:, 1, h, :], start=False, stop=True)
                last.then_inc(av_done, 1)

            def turn_max(i, s, t):
                pe.wait_ge(max_done, i * 12 + (12 if t else 4))
                nc.tensor.transpose(side_bank[0:H, 0:P], neg_max[:, t],
                                    c["ident"][:, :]).then_inc(max_t_ready, 1)

            def step(i, s):
                S, X, F, T = 0 <= s < NSEQ, 0 <= s - 1 < NSEQ, 0 <= s + 1 < NSEQ, 0 <= s - 2 < NSEQ
                n = i + 2
                for j in range(6):
                    if j == 0 and S:
                        pe.wait_ge(rows_in, (i + 1) * 16 * LOADS)
                    if S:
                        scores(i, s, 2 * j)
                        scores(i, s, 2 * j + 1)
                    if j == 0 and X:
                        at_least(pe, v_copied, min(i, NSEQ - 1) + 1 if isinstance(i, int) else i + 1)
                        at_least(pe, proj_added, i - 2)
                        turn_max(i - 1, s - 1, 1)
                    if j == 2 and F:
                        pe.wait_ge(f_copied, n)
                        nc.tensor.matmul(q_ps, wq_gdu[:, :], xt[:, :], start=True, stop=True)
                        nc.tensor.matmul(k_ps, wk_gdu[:, :], xt[:, :], start=True, stop=True).then_inc(qk_ready, 1)
                    if j == 3 and S:
                        if F:
                            pe.wait_ge(qk_lo_done, n * 2)
                        else:
                            pe.wait_ge(max_t_copied, i * 2)
                        turn_max(i, s, 0)
                    if j == 4 and F:
                        if S:
                            pe.wait_ge(max_t_copied, i * 2 + 1)
                        else:
                            pe.wait_ge(qk_lo_done, n * 2)
                        for t in range(2):
                            last = nc.tensor.matmul(side_bank[:, t * D:(t + 1) * D], xt[:, t * P:(t + 1) * P], c["Wv"][:, :],
                                                    start=True, stop=True)
                        last.then_inc(v_ready, 1)
                    if X:
                        turned_scores(i - 1, s - 1, j)
                    if j == 4 and T:
                        if F:
                            pe.wait_ge(v_copied, n)
                        elif X:
                            pe.wait_ge(max_t_copied, i * 2 + (1 if S else 0))
                        pe.wait_ge(attn_done, i - 1)
                        for t in range(2):
                            last = nc.tensor.transpose(side_bank[:, t * P:(t + 1) * P],
                                                       attn[:, t * H:(t + 1) * H, :].rearrange("p h d -> p (h d)"), c["ident"][:, :])
                        last.then_inc(attn_t_ready, 1)
                    if j == 0 and F:
                        if X:
                            pe.wait_ge(max_t_copied, i * 2)
                        else:
                            at_least(pe, v_copied, i + 1)
                        pe.wait_ge(xn_done, n)
                        for t in range(2):
                            last = nc.tensor.transpose(side_bank[:, t * P:(t + 1) * P], xn[:, t], c["ident"][:, :])
                        last.then_inc(xt_ready, 1)
                    if j == 1 and F:
                        pe.wait_ge(xt_copied, n)
                        nc.tensor.matmul(side_bank[0:H, 0:N], c["Wf"][:, :], xt[:, :], start=True, stop=True).then_inc(f_ready, 1)
                    if j < 2 and T:
                        times_v(i - 2, s - 2, j + 4)
                    if j >= 2 and X:
                        times_v(i - 1, s - 1, j - 2)
                    if j == 5 and T:
                        pe.wait_ge(attn_t_copied, i - 1)
                        for t in range(2):
                            last = nc.tensor.matmul(side_bank[:, t * D:(t + 1) * D], attn_t[:, t * P:(t + 1) * P], c["Wo"][:, :],
                                                    start=True, stop=True)
                        last.then_inc(proj_ready, 1)
            steps(pe, step)


def program(nc, x, Wq, Wk, Wv, Wo, Wf, Wg, We, be, out):
    B, N, D = x.shape
    H, E = Wf.shape[1], Wg.shape[1]
    T = B * N // P
    x_rows = x.rearrange("b n d -> (b n) d")
    out_rows = out.rearrange("b n d -> (b n) d")
    with ExitStack() as ctx:
        sb = lambda name, shape, dt: ctx.enter_context(nc.sbuf_tensor(name, shape, dt))
        banks = [ctx.enter_context(nc.psum_tensor(f"bank{i}", [P, BANK], FP32)) for i in range(8)]
        x_all = sb("x_all", [P, T, D], FP32)
        c = {
            "E": E, "H": H,
            "we": sb("we", [P, E, D], FP32), "wg": sb("wg", [P, E], FP32),
            "Wq": sb("wq", [P, D], FP32), "Wk": sb("wk", [P, D], FP32), "Wv": sb("wv", [P, D], FP32),
            "Wo": sb("wo", [P, D], FP32), "Wf": sb("wf", [P, H], FP32),
            "we_hi": sb("we_hi", [P, E * D], FP32R), "we_lo": sb("we_lo", [P, E * D], FP32R),
            "wg_hi": sb("wg_hi", [P, E], FP32R), "wg_lo": sb("wg_lo", [P, E], FP32R),
            "bias": sb("bias", [96, 4 * D], FP32), "bias_split": sb("bias_split", [96, 4 * D], FP32R),
            "ident": sb("ident", [P, P], FP32), "expert_no": sb("expert_no", [P, E], FP32),
            "minus_half": sb("minus_half", [P, 4], FP32),
        }
        w = {"Wq": Wq, "Wk": Wk, "Wv": Wv, "Wo": Wo, "Wf": Wf, "Wg": Wg, "We": We, "be": be}
        load_constants(nc, sb, w, c)
        moe_layer(nc, c, banks, x_all, "m1_", x_dram=x_rows)
        attention_layer(nc, c, banks, x_all, N)
        moe_layer(nc, c, banks, x_all, "m2_", out_dram=out_rows)


_INS = ["L0_attn_x", "L0_attn_Wq", "L0_attn_Wk", "L0_attn_Wv", "L0_attn_Wo", "L0_attn_Wf",
        "L0_ffn_Wg", "L0_ffn_We", "L0_ffn_be"]


def kernel(**inputs):
    import numpy as _np
    import concourse.bacc as _bacc
    from concourse import mybir as _mybir
    from concourse.bass_utils import run_bass_kernel_spmd as _run

    nc = _bacc.Bacc("TRN2", target_bir_lowering=False, num_devices=1)
    arrays, args = {}, []
    for name in _INS:
        a = _np.ascontiguousarray(inputs[name])
        arrays[f"in_{name}"] = a
        args.append(nc.dram_tensor(f"in_{name}", a.shape, _mybir.dt.from_np(a.dtype), kind="ExternalInput").ap())
    x = arrays["in_L0_attn_x"]
    args.append(nc.dram_tensor("out_x", x.shape, _mybir.dt.from_np(x.dtype), kind="ExternalOutput").ap())
    program(nc, *args)
    r = _run(nc, [arrays], core_ids=[0])
    return r.results[0]["out_x"]
```

```python
import concourse.bass as bass
from concourse import mybir
from contextlib import ExitStack

FP32 = mybir.dt.float32
FP32R = mybir.dt.float32r
BF16 = mybir.dt.bfloat16
U32 = mybir.dt.uint32
ALU = mybir.AluOpType
ACT = mybir.ActivationFunctionType
AX = mybir.AxisListType

P = 128
EPS = 1e-5
BANK = 512


def at_least(eng, sem, value):
    if isinstance(value, int) and value <= 0:
        return
    eng.wait_ge(sem, value)


def wait_apart(eng, sem, value, counted):
    eng.wait_ge(sem, value)
    eng.sem_inc(counted, 1)


def run_steps(eng, step, first, last, body, unroll):
    lo, hi = body
    for i in range(first, lo):
        step(i, i)
    with eng.Fori(0, (hi - lo) // unroll) as k:
        for part in range(unroll):
            step(k * unroll + (lo + part), lo + part)
    for i in range(hi, last):
        step(i, i)


def load_constants(nc, sb, w, c):
    with ExitStack() as ctx:
        sem = lambda name: ctx.enter_context(nc.semaphore(name))
        loaded, bias_loaded, filled = sem("weights_loaded"), sem("bias_loaded"), sem("filled")
        zeroed = sem("bias_zeroed")
        split_hi, pool_made = sem("split_hi"), sem("pool_made")
        block = ctx.enter_context(nc.Block())
        E, D = c["E"], P

        @block.sync
        def _(sp):
            sp.dma_start(c["we"][:, :, :], w["We"].rearrange("e h d -> h e d")).then_inc(loaded, 16)
            sp.dma_start(c["wg"][:, :], w["Wg"]).then_inc(loaded, 16)
            for name in ("Wq", "Wk", "Wv", "Wo"):
                sp.dma_start(c[name][:, :], w[name]).then_inc(loaded, 16)
            sp.dma_start(c["Wf"][:, :], w["Wf"]).then_inc(loaded, 16)
            sp.wait_ge(zeroed, 1)
            for part in range(3):
                for q in range(4):
                    row = 32 * part + q * E
                    sp.dma_start(c["bias"][row:row + E, q * D:(q + 1) * D], w["be"]).then_inc(bias_loaded, 16)

        @block.gpsimd
        def _(pool):
            nc.gpsimd.memset(c["ident"][:, :], 0.0).then_inc(filled, 1)
            nc.gpsimd.memset(c["bias"][:, :], 0.0).then_inc(zeroed, 1)
            pool.wait_ge(filled, 1)
            nc.gpsimd.affine_select(out=c["ident"][:, :], in_=c["ident"][:, :], compare_op=ALU.not_equal, fill=1.0,
                                    base=0, pattern=[[-1, P]], channel_multiplier=1).then_inc(filled, 1)
            nc.gpsimd.iota(c["expert_no"][:, :], pattern=[[1, E]], base=0, channel_multiplier=0,
                           allow_small_or_imprecise_dtypes=True).then_inc(pool_made, 1)
            nc.gpsimd.memset(c["minus_half"][:, :], -0.5).then_inc(pool_made, 1)

        @block.scalar
        def _(act):
            nc.scalar.preload_act_table_set("natural_log_exp_and_others")
            act.wait_ge(loaded, 16 * 7)
            nc.scalar.activation(c["we_hi"][:, :], c["we"][:, :, :].rearrange("p e d -> p (e d)"), ACT.Copy).then_inc(split_hi, 1)
            nc.scalar.activation(c["wg_hi"][:, :], c["wg"][:, :], ACT.Copy).then_inc(split_hi, 1)

        @block.vector
        def _(dve):
            dve.wait_ge(split_hi, 2)
            nc.vector.tensor_tensor(c["we_lo"][:, :], c["we"][:, :, :].rearrange("p e d -> p (e d)"),
                                    c["we_hi"][:, :].bitcast(FP32), ALU.subtract)
            nc.vector.tensor_tensor(c["wg_lo"][:, :], c["wg"][:, :], c["wg_hi"][:, :].bitcast(FP32), ALU.subtract)
            dve.wait_ge(bias_loaded, 16 * 12)
            nc.vector.tensor_copy(c["bias_split"][:, :], c["bias"][:, :]).then_inc(split_hi, 1)
            dve.wait_ge(split_hi, 3)
            nc.vector.tensor_tensor(c["bias_split"][64:96, :], c["bias"][64:96, :],
                                    c["bias_split"][64:96, :].bitcast(FP32), ALU.subtract)


def moe_layer(nc, c, banks, x_all, tag, x_dram=None, out_dram=None):
    E, Q, G = c["E"], 4, x_all.shape[1] // 4
    D = P
    with ExitStack() as ctx:
        sb = lambda name, shape, dt: ctx.enter_context(nc.sbuf_tensor(tag + name, shape, dt))
        sem = lambda name: ctx.enter_context(nc.semaphore(tag + name))
        stats = sb("stats", [P, 2, Q, 6], FP32)
        moments = sb("moments", [P, 2, Q, 2], FP32)
        var_eps = sb("var_eps", [P, 2, Q], FP32)
        rstd = sb("rstd", [P, 2, Q], FP32)
        xn = sb("xn", [P, 2, Q, D], FP32)
        xt_hi = sb("xt_hi", [P, 2, Q * P], FP32R)
        xt_lo = sb("xt_lo", [P, 2, Q * P], FP32R)
        best = sb("best", [P, Q, 8], FP32)
        best_no = sb("best_no", [P, Q, 8], U32)
        gap = sb("gap", [P, Q], FP32)
        egap = sb("egap", [P, Q], FP32)
        denom = sb("denom", [P, Q], FP32)
        g1 = sb("g1", [P, Q], FP32)
        g2 = sb("g2", [P, Q], FP32)
        hot1 = sb("hot1", [P, Q, E], FP32)
        hot2 = sb("hot2", [P, Q, E], FP32)
        gates = sb("gates", [P, 2, Q, E], FP32)
        gates3 = sb("gates3", [P, 3, Q * E], FP32R)
        gates_t = sb("gates_t", [3 * Q * E, P], FP32R)
        scaled = sb("scaled", [P, 2, 4, D], FP32)
        pair = sb("pair", [P, 2, 2, D], FP32)
        upper = sb("upper", [P, 2, D], FP32)
        lower = sb("lower", [P, 2, 4, D], FP32)

        y_low = [banks[0], banks[2]]
        y_high = [banks[1], banks[3]]
        xt_bank = banks[4]
        gate_bank = banks[5]
        gates_t_bank = banks[6]
        bias_bank = banks[7]
        logits = gate_bank[:, 0:Q * E].rearrange("p (q e) -> p q e", e=E)

        x_in = sem("x_in")
        stat_done, mom_done, eps_done = sem("stat_done"), sem("mom_done"), sem("eps_done")
        rstd_done, xn_done = sem("rstd_done"), sem("xn_done")
        xt_ready, hi_ready, lo_ready = sem("xt_ready"), sem("hi_ready"), sem("lo_ready")
        logits_ready, chain = sem("logits_ready"), sem("gate_chain")
        no_ready, gap_ready, egap_ready = sem("no_ready"), sem("gap_ready"), sem("egap_ready")
        gates_ready, gates_t_ready, gates_t_copied = sem("gates_ready"), sem("gates_t_ready"), sem("gates_t_copied")
        bias_ready, bias_added = sem("bias_ready"), sem("bias_added")
        y_ready, high_used = sem("y_ready"), sem("high_used")
        low_chain, pair_done, upper_done, upper_used = sem("low_chain"), sem("pair_done"), sem("upper_done"), sem("upper_used")
        stored, waited = sem("stored"), sem("waited")
        CH = 8
        block = ctx.enter_context(nc.Block())

        def steps(eng, step):
            run_steps(eng, step, -2, G, (2, G - 2), 2)

        @block.sync
        def _(sp):
            if x_dram is not None:
                load = lambda g: sp.dma_start(
                    x_all[:, bass.ds(g * Q, Q), :],
                    x_dram[bass.ds(g * (Q * P), Q * P), :].rearrange("(q p) d -> p q d", p=P)).then_inc(x_in, 16)
                load(0)
                with sp.Fori(1, G) as g:
                    sp.wait_ge(x_in, g * 16)
                    load(g)
            if out_dram is not None:
                with sp.Fori(0, G) as g:
                    sp.wait_ge(upper_used, g * Q + Q)
                    sp.dma_start(out_dram[bass.ds(g * (Q * P), Q * P), :].rearrange("(q p) d -> p q d", p=P),
                                 x_all[:, bass.ds(g * Q, Q), :]).then_inc(stored, 16)
                sp.wait_ge(stored, 16 * G)

        @block.gpsimd
        def _(pool):
            def step(i, s):
                b = s % 2
                if 0 <= s:
                    for q in range(Q):
                        t = i * Q + q
                        pool.wait_ge(high_used, t + 1)
                        nc.gpsimd.tensor_tensor(pair[:, q % 2], scaled[:, q % 2, 0:2], scaled[:, q % 2, 2:4],
                                                ALU.add).then_inc(pair_done, 1)
                        pool.wait_ge(pair_done, t + 1)
                        at_least(pool, upper_used, t - 1)
                        nc.gpsimd.tensor_tensor(upper[:, q % 2], pair[:, q % 2, 0], pair[:, q % 2, 1],
                                                ALU.add).then_inc(upper_done, 1)
                if s + 2 < G:
                    pool.wait_ge(eps_done, i + 3)
                    nc.gpsimd.tensor_tensor(rstd[:, b], var_eps[:, b], c["minus_half"][:, 0:Q],
                                            ALU.pow).then_inc(rstd_done, 1)
            steps(pool, step)

        @block.scalar
        def _(act):
            def experts(i, s, q):
                t = i * Q + q
                act.wait_ge(y_ready, t + 1)
                at_least(act, pair_done, t - 1)
                for j in range(4):
                    last = nc.scalar.activation(scaled[:, q % 2, j], y_high[q % 2][:, j * D:(j + 1) * D], ACT.Copy,
                                                scale=gates[:, s % 2, q, 4 + j:5 + j])
                last.then_inc(high_used, 1)

            def step(i, s):
                a, n = (s + 1) % 2, i + 2
                A, B = -1 <= s and s + 1 < G, 0 <= s
                if A:
                    act.wait_ge(xt_ready, n)
                    nc.scalar.activation(xt_hi[:, a], xt_bank[:, :], ACT.Copy).then_inc(hi_ready, 1)
                if B:
                    experts(i, s, 0)
                    experts(i, s, 1)
                if A:
                    act.wait_ge(gap_ready, n)
                    nc.scalar.activation(egap[:, :], gap[:, :], ACT.Exp).then_inc(egap_ready, 1)
                if B:
                    experts(i, s, 2)
                if A:
                    act.wait_ge(gates_t_ready, n)
                    nc.scalar.activation(gates_t[:, :], gates_t_bank[0:3 * Q * E, 0:P], ACT.Copy).then_inc(gates_t_copied, 1)
                if B:
                    experts(i, s, 3)
            steps(act, step)

        @block.vector
        def _(dve):
            def normalise(i, s):
                b, n, g = s % 2, i + 3, i + 2
                if x_dram is not None:
                    dve.wait_ge(x_in, n * 16)
                for q in range(Q):
                    last = nc.vector.bn_stats(stats[:, b, q], x_all[:, bass.ds(g * Q + q, 1), :].rearrange("p a d -> p (a d)"))
                last.then_inc(stat_done, 1)
                wait_apart(dve, stat_done, n, waited)
                for q in range(Q):
                    last = nc.vector.bn_aggr(moments[:, b, q], stats[:, b, q])
                last.then_inc(mom_done, 1)
                dve.wait_ge(mom_done, n)
                nc.vector.tensor_scalar(var_eps[:, b], moments[:, b, :, 1], EPS, None, ALU.add).then_inc(eps_done, 1)

            def normalise2(i, s):
                b, n, g = s % 2, i + 3, i + 2
                dve.wait_ge(rstd_done, n)
                for q in range(Q):
                    last = nc.vector.tensor_scalar(xn[:, b, q], x_all[:, bass.ds(g * Q + q, 1), :].rearrange("p a d -> p (a d)"),
                                                   moments[:, b, q, 0:1], rstd[:, b, q:q + 1], ALU.subtract, ALU.mult)
                last.then_inc(xn_done, 1)

            def low_part(i, s):
                a, n = (s + 1) % 2, i + 2
                dve.wait_ge(hi_ready, n)
                nc.vector.tensor_tensor(xt_lo[:, a], xt_bank[:, :], xt_hi[:, a].bitcast(FP32), ALU.subtract).then_inc(lo_ready, 1)

            def link(n, k, ins):
                ins.then_inc(chain, 1)
                dve.wait_ge(chain, (n - 1) * CH + k)

            def pick(i, s):
                n = i + 2
                wait_apart(dve, logits_ready, n, waited)
                for q in range(Q):
                    last = nc.vector.max(best[:, q], logits[:, q])
                link(n, 1, last)
                nc.vector.tensor_tensor(gap[:, :], best[:, :, 1], best[:, :, 0], ALU.subtract).then_inc(gap_ready, 1)
                for q in range(Q):
                    last = nc.vector.max_index(best_no[:, q], best[:, q], logits[:, q])
                last.then_inc(no_ready, 1)
                every = c["expert_no"][:, :].unsqueeze(1).broadcast_to([P, Q, E])
                dve.wait_ge(no_ready, n)
                nc.vector.tensor_tensor(hot1[:, :, :], every, best_no[:, :, 0:1].broadcast_to([P, Q, E]), ALU.is_equal)
                link(n, 2, nc.vector.tensor_tensor(hot2[:, :, :], every, best_no[:, :, 1:2].broadcast_to([P, Q, E]), ALU.is_equal))

            def weigh(i, s):
                a, n = (s + 1) % 2, i + 2
                dve.wait_ge(egap_ready, n)
                link(n, 3, nc.vector.tensor_scalar(denom[:, :], egap[:, :], 2.0, 2.0, ALU.mult, ALU.add))
                link(n, 4, nc.vector.reciprocal(g1[:, :], denom[:, :]))
                nc.vector.tensor_tensor(hot1[:, :, :], hot1[:, :, :], g1[:, :].unsqueeze(2).broadcast_to([P, Q, E]), ALU.mult)
                link(n, 5, nc.vector.tensor_tensor(g2[:, :], egap[:, :], g1[:, :], ALU.mult))
                link(n, 6, nc.vector.tensor_tensor(hot2[:, :, :], hot2[:, :, :], g2[:, :].unsqueeze(2).broadcast_to([P, Q, E]), ALU.mult))
                link(n, 7, nc.vector.tensor_tensor(gates[:, a], hot1[:, :, :], hot2[:, :, :], ALU.add))
                flat = gates[:, a].rearrange("p q e -> p (q e)")
                nc.vector.tensor_copy(gates3[:, 0], flat)
                link(n, 8, nc.vector.tensor_copy(gates3[:, 2], flat))
                nc.vector.tensor_tensor(gates3[:, 1], flat, gates3[:, 0].bitcast(FP32), ALU.subtract).then_inc(gates_ready, 1)

            def experts(i, s, q):
                t = i * Q + q
                x_t = x_all[:, bass.ds(t, 1), :].rearrange("p a d -> p (a d)")
                dve.wait_ge(y_ready, t + 1)
                before = x_t
                for j in range(4):
                    ins = nc.vector.scalar_tensor_tensor(out=lower[:, q % 2, j], in0=y_low[q % 2][:, j * D:(j + 1) * D],
                                                         scalar=gates[:, s % 2, q, j:j + 1], in1=before,
                                                         op0=ALU.mult, op1=ALU.add)
                    before = lower[:, q % 2, j]
                    ins.then_inc(low_chain, 1)
                    dve.wait_ge(low_chain, t * 4 + (j + 1))
                dve.wait_ge(upper_done, t + 1)
                nc.vector.tensor_tensor(x_t, before, upper[:, q % 2], ALU.add).then_inc(upper_used, 1)

            def step(i, s):
                A, B = -1 <= s and s + 1 < G, 0 <= s
                if B:
                    dve.wait_ge(bias_ready, i + 1)
                    xg = x_all[:, bass.ds(i * Q, Q), :].rearrange("p q d -> p (q d)")
                    nc.vector.tensor_tensor(xg, xg, bias_bank[:, :], ALU.add).then_inc(bias_added, 1)
                    dve.wait_ge(bias_added, i + 1)
                if A:
                    low_part(i, s)
                if B:
                    experts(i, s, 0)
                if A:
                    pick(i, s)
                if B:
                    experts(i, s, 1)
                if A:
                    weigh(i, s)
                if B:
                    experts(i, s, 2)
                if s + 2 < G:
                    normalise(i, s)
                if B:
                    experts(i, s, 3)
                if s + 2 < G:
                    normalise2(i, s)
            steps(dve, step)

        @block.tensor
        def _(pe):
            def experts(i, s, q):
                t = i * Q + q
                b = s % 2
                at_least(pe, low_chain, (t - 1) * 4)
                at_least(pe, high_used, t - 1)
                hi, lo = xt_hi[:, b, q * P:(q + 1) * P], xt_lo[:, b, q * P:(q + 1) * P]
                H = 4 * D
                for k, (x_part, w_part) in enumerate(((hi, c["we_hi"]), (hi, c["we_lo"]), (lo, c["we_hi"]))):
                    nc.tensor.matmul(y_low[q % 2][:, :], x_part, w_part[:, 0:H], start=k == 0, stop=k == 2)
                    last = nc.tensor.matmul(y_high[q % 2][:, :], x_part, w_part[:, H:2 * H], start=k == 0, stop=k == 2)
                last.then_inc(y_ready, 1)

            def step(i, s):
                a, n = (s + 1) % 2, i + 2
                A, B = -1 <= s and s + 1 < G, 0 <= s
                if A:
                    pe.wait_ge(xn_done, n)
                    at_least(pe, lo_ready, n - 1)
                    for q in range(Q):
                        last = nc.tensor.transpose(xt_bank[:, q * P:(q + 1) * P], xn[:, a, q], c["ident"][:, :])
                    last.then_inc(xt_ready, 1)
                if B:
                    experts(i, s, 0)
                if A:
                    pe.wait_ge(lo_ready, n)
                    for q in range(Q):
                        hi, lo = xt_hi[:, a, q * P:(q + 1) * P], xt_lo[:, a, q * P:(q + 1) * P]
                        nc.tensor.matmul(logits[:, q], hi, c["wg_hi"][:, :], start=True, stop=False)
                        nc.tensor.matmul(logits[:, q], hi, c["wg_lo"][:, :], start=False, stop=False)
                        last = nc.tensor.matmul(logits[:, q], lo, c["wg_hi"][:, :], start=False, stop=True)
                    last.then_inc(logits_ready, 1)
                if B:
                    experts(i, s, 1)
                    experts(i, s, 2)
                if A:
                    pe.wait_ge(gates_ready, n)
                    nc.tensor.transpose(gates_t_bank[0:3 * Q * E, 0:P], gates3[:, :, :].rearrange("p k n -> p (k n)").bitcast(FP32),
                                        c["ident"][:, :]).then_inc(gates_t_ready, 1)
                if B:
                    experts(i, s, 3)
                if A:
                    pe.wait_ge(gates_t_copied, n)
                    at_least(pe, bias_added, n - 1)
                    nc.tensor.matmul(bias_bank[:, :], gates_t[:, :], c["bias_split"][:, :],
                                     start=True, stop=True).then_inc(bias_ready, 1)
            steps(pe, step)


def attention_layer(nc, c, banks, x_all, S_LEN):
    H, D = c["H"], P
    NSEQ = x_all.shape[1] // 2
    HD = D // H
    NG, NU = 4, H // 4
    ROWS = 3 * HD + 2
    KR = NG * ROWS
    KM = KR + 2
    SCALE = float(HD) ** -0.5
    N = S_LEN
    with ExitStack() as ctx:
        sb = lambda name, shape, dt: ctx.enter_context(nc.sbuf_tensor("a_" + name, shape, dt))
        sem = lambda name: ctx.enter_context(nc.semaphore("a_" + name))
        stats = sb("stats", [P, 2, 6], FP32)
        moments = sb("moments", [P, 2, 2], FP32)
        var_eps = sb("var_eps", [P, 2], FP32)
        rstd = sb("rstd", [P, 2], FP32)
        xn = sb("xn", [P, 2, D], FP32)
        xt = sb("xt", [P, N], FP32)
        f = sb("f", [H, N], FP32)
        neg_abs = sb("neg_abs", [H, N], FP32)
        exp_f = sb("exp_f", [H, N], FP32)
        log_f = sb("log_f", [H, N], FP32)
        log_sig = sb("log_sig", [H, N], FP32)
        neg_c = sb("neg_c", [H, N], FP32)
        c_parts = sb("c_parts", [H, 2, N], FP32R)
        wq_gdu = sb("wq_gdu", [P, D], FP32)
        wk_gdu = sb("wk_gdu", [P, D], FP32)
        ones_row = sb("ones_row", [H, N], FP32)
        zero_row = sb("zero_row", [H, N], FP32)
        ones_r = sb("ones_r", [2, NU * N], FP32R)
        q_parts = sb("q_parts", [P, 2, N], FP32R)
        k_parts = sb("k_parts", [P, 2, N], FP32R)
        q_rows = [sb(f"q_rows{b}", [KM, H, N], FP32R) for b in range(3)]
        k_rows = [sb(f"k_rows{b}", [KM, NU, N], FP32R) for b in range(3)]
        v_sb = [sb(f"v{b}", [P, 2, H, 32], FP32) for b in range(3)]
        neg_max = sb("neg_max", [P, 2, H], FP32)
        max_t = [sb(f"max_t{t}", [H, 2, P], FP32R) for t in range(2)]
        weights = [sb(f"weights{n}", [P, 8, P], FP32) for n in range(3)]
        out_t = sb("out_t", [P, 2, NU * P], FP32)
        recip = sb("recip", [P, 2, H], FP32)
        attn = sb("attn", [P, 2, H, HD], FP32)
        attn_t = sb("attn_t", [P, N], FP32)
        ident16 = sb("ident16", [P, P], BF16)
        mask16 = sb("mask16", [P, 4, P], BF16)
        mask16_t = sb("mask16_t", [P, 4, P], BF16)

        score_bank = banks[0:2]
        wt_bank = banks[2:4]
        out_bank = banks[4:6]
        side_bank = banks[6]
        proj_bank = banks[7]
        q_ps, k_ps = proj_bank[:, 0:N], proj_bank[:, N:2 * N]

        set_up, zeroed, ones_in = sem("set_up"), sem("zeroed"), sem("ones_in")
        stat_done, mom_done, eps_done = sem("stat_done"), sem("mom_done"), sem("eps_done")
        rstd_done, xn_done = sem("rstd_done"), sem("xn_done")
        xt_ready, xt_copied = sem("xt_ready"), sem("xt_copied")
        f_ready, f_copied, neg_abs_done = sem("f_ready"), sem("f_copied"), sem("neg_abs_done")
        exp_done, log_done, log_sig_done = sem("exp_done"), sem("log_done"), sem("log_sig_done")
        c_done, c_hi_done, c_lo_done = sem("c_done"), sem("c_hi_done"), sem("c_lo_done")
        qk_ready, qk_hi_done, qk_lo_done = sem("qk_ready"), sem("qk_hi_done"), sem("qk_lo_done")
        v_ready, v_copied = sem("v_ready"), sem("v_copied")
        rows_in = sem("rows_in")
        scores_ready, max_done = sem("scores_ready"), sem("max_done")
        max_t_ready, max_hi_done, max_lo_done = sem("max_t_ready"), sem("max_hi_done"), sem("max_lo_done")
        max_in = [sem("max_in0"), sem("max_in1")]
        wt_ready, wt_exp, av_done = sem("wt_ready"), sem("wt_exp"), sem("av_done")
        out_copied, turned_ready = sem("out_copied"), sem("turned_ready")
        recip_done, attn_done = sem("recip_done"), sem("attn_done")
        attn_t_ready, attn_t_copied = sem("attn_t_ready"), sem("attn_t_copied")
        proj_ready, proj_added = sem("proj_ready"), sem("proj_added")
        dve_waited, sp_waited = sem("dve_waited"), sem("sp_waited")
        k_stored, q_stored, c_stored, w_ordered = sem("k_stored"), sem("q_stored"), sem("c_stored"), sem("w_ordered")
        LOADS = NG + 1
        raw = lambda tile: tile[(slice(None),) * len(tile.shape)].bitcast(FP32)
        q_dram = nc.dram_tensor("q_stage", (3, NG, 3 * HD, NU, N), FP32, kind="Internal").ap()
        k_dram = nc.dram_tensor("k_stage", (3, NG, ROWS, NU, N), FP32, kind="Internal").ap()
        block = ctx.enter_context(nc.Block())

        def steps(eng, step):
            run_steps(eng, step, -2, NSEQ + 2, (2, 2 + (NSEQ - 4) // 3 * 3), 3)

        @block.sync
        def _(sp):
            sp.wait_ge(zeroed, 1)
            ones = ones_r[:, :].bitcast(FP32).rearrange("r (u n) -> r u n", u=NU)
            for b in range(3):
                for g in range(NG):
                    sp.dma_start(raw(q_rows[b])[ROWS * g + 3 * HD:ROWS * (g + 1), NU * g:NU * (g + 1), :], ones).then_inc(ones_in, 16)
                sp.dma_start(raw(k_rows[b])[KR:KM, :, :], ones).then_inc(ones_in, 16)

            def max_rows(i, s, t):
                for part, parts_done in enumerate((max_hi_done, max_lo_done)):
                    sp.wait_ge(parts_done, i * 2 + t + 1)
                    sp.dma_start(raw(q_rows[s % 3])[KR + part:KR + part + 1, :, t * P:(t + 1) * P],
                                 raw(max_t[t])[:, part, :]).then_inc(max_in[t], 16)

            def step(i, s):
                if 0 <= s - 1 < NSEQ:
                    max_rows(i - 1, s - 1, 1)
                if 0 <= s + 1 < NSEQ:
                    b, n = (s + 1) % 3, i + 2
                    if 0 <= s:
                        wait_apart(sp, scores_ready, i * 12 + 1, sp_waited)
                    at_least(sp, wt_ready, (i - 1) * 12)
                    sp.wait_ge(q_stored, n * 16 * 3)
                    for g in range(NG):
                        sp.dma_start(raw(q_rows[b])[ROWS * g:ROWS * g + 3 * HD, NU * g:NU * (g + 1), :],
                                     q_dram[b, g]).then_inc(rows_in, 16)
                    wait_apart(sp, k_stored, n * 16 * 3, sp_waited)
                    sp.wait_ge(c_stored, n * 16 * 2)
                    sp.dma_start(raw(k_rows[b])[0:KR, :, :], k_dram[b].rearrange("g r u n -> (g r) u n")).then_inc(rows_in, 16)
                if 0 <= s < NSEQ:
                    max_rows(i, s, 0)
                if 0 <= s + 2 < NSEQ:
                    b, n = (s + 2) % 3, i + 3
                    sp.wait_ge(qk_lo_done, n * 2)
                    for r, part in enumerate((0, 1, 0)):
                        sp.dma_start(k_dram[b, :, r * HD:(r + 1) * HD].rearrange("g d u n -> g (d u) n"),
                                     raw(k_parts)[:, part, :]).then_inc(k_stored, 16)
                    for r, part in enumerate((0, 0, 1)):
                        sp.dma_start(q_dram[b, :, r * HD:(r + 1) * HD].rearrange("g d u n -> g (d u) n"),
                                     raw(q_parts)[:, part, :]).then_inc(q_stored, 16)
                    sp.wait_ge(c_lo_done, n)
                    for part in range(2):
                        sp.dma_start(k_dram[b, :, 3 * HD + part], raw(c_parts)[:, part, :]).then_inc(c_stored, 16)
            steps(sp, step)

        @block.gpsimd
        def _(pool):
            for b in range(3):
                last = nc.gpsimd.memset(q_rows[b][:, :, :].bitcast(U32), 0)
            nc.gpsimd.memset(ones_r[:, :].bitcast(FP32), 1.0).then_inc(zeroed, 1)
            for b in range(3):
                nc.gpsimd.memset(v_sb[b][:, :, :, HD + 1:], 0.0)
                nc.gpsimd.memset(v_sb[b][:, :, :, HD:HD + 1], 1.0)
            nc.gpsimd.memset(ones_row[:, :], 1.0)
            nc.gpsimd.memset(zero_row[:, :], 0.0)
            nc.gpsimd.memset(ident16[:, :], 0.0)
            nc.gpsimd.memset(mask16_t[:, :, :], 0.0)
            nc.gpsimd.memset(mask16[:, :, :], 0.0).then_inc(set_up, 1)
            pool.wait_ge(set_up, 1)
            nc.gpsimd.affine_select(out=ident16[:, :], in_=ident16[:, :], compare_op=ALU.not_equal, fill=1.0,
                                    base=0, pattern=[[-1, P]], channel_multiplier=1)
            nc.gpsimd.affine_select(out=mask16_t[:, :, :], in_=mask16_t[:, :, :], compare_op=ALU.is_ge, fill=-1e30,
                                    base=0, pattern=[[0, 4], [1, P]], channel_multiplier=-1)
            nc.gpsimd.affine_select(out=mask16[:, :, :], in_=mask16[:, :, :], compare_op=ALU.is_ge, fill=-1e30,
                                    base=0, pattern=[[0, 4], [-1, P]], channel_multiplier=1).then_inc(set_up, 1)

            def step(i, s):
                if 0 <= s + 2 < NSEQ:
                    n = i + 3
                    pool.wait_ge(eps_done, n)
                    nc.gpsimd.tensor_tensor(rstd[:, :], var_eps[:, :], c["minus_half"][:, 0:2], ALU.pow).then_inc(rstd_done, 1)
                    pool.wait_ge(c_done, n)
                    at_least(pool, c_stored, (n - 1) * 16 * 2)
                    nc.gpsimd.tensor_tensor(c_parts[:, 0], neg_c[:, :], zero_row[:, :], ALU.add).then_inc(c_hi_done, 1)
                    pool.wait_ge(c_hi_done, n)
                    nc.gpsimd.tensor_tensor(c_parts[:, 1], neg_c[:, :], c_parts[:, 0].bitcast(FP32), ALU.subtract).then_inc(c_lo_done, 1)
            steps(pool, step)

        @block.scalar
        def _(act):
            def copy_max(i, s, t):
                act.wait_ge(max_t_ready, i * 2 + t + 1)
                at_least(act, max_in[t], i * 32)
                nc.scalar.activation(max_t[t][:, 0], side_bank[0:H, 0:P], ACT.Copy).then_inc(max_hi_done, 1)

            def exp(i, s, n):
                act.wait_ge(wt_ready, i * 12 + n + 1)
                if n % 2 == 0:
                    at_least(act, av_done, i * 6 + n // 2 - 2)
                half = 4 * (n % 2)
                nc.scalar.activation(weights[n // 2 % 3][:, half:half + 4, :].rearrange("p h n -> p (h n)"),
                                     wt_bank[n % 2][:, :], ACT.Exp).then_inc(wt_exp, 1)

            def copy_out(i, s, t):
                act.wait_ge(av_done, i * 6 + (6 if t else 2))
                nc.scalar.activation(out_t[:, t], out_bank[t][:, :], ACT.Copy).then_inc(out_copied, 1)

            nc.scalar.preload_act_table_set("natural_log_exp_and_others")
            for made, name in ((wq_gdu, "Wq"), (wk_gdu, "Wk")):
                nc.scalar.activation(made[:, :].rearrange("p (g d u) -> p g d u", g=NG, u=NU),
                                     c[name][:, :].rearrange("p (g u d) -> p g d u", g=NG, u=NU), ACT.Copy).then_inc(w_ordered, 1)

            def step(i, s):
                S, X, T = 0 <= s < NSEQ, 0 <= s - 1 < NSEQ, 0 <= s - 2 < NSEQ
                V, F, n = 0 <= s + 1 < NSEQ, 0 <= s + 2 < NSEQ, i + 3
                for j in range(6):
                    if j == 0 and X:
                        copy_max(i - 1, s - 1, 1)
                    if j == 2 and V:
                        act.wait_ge(v_ready, i + 2)
                        at_least(act, av_done, (i - 1) * 6)
                        nc.scalar.activation(v_sb[(s + 1) % 3][:, :, :, 0:HD].rearrange("p t h d -> p (t h) d"),
                                             side_bank[:, 0:2 * D].rearrange("p (n d) -> p n d", d=HD), ACT.Copy).then_inc(v_copied, 1)
                    if j == 3 and S:
                        copy_max(i, s, 0)
                    if j == 3 and F:
                        act.wait_ge(f_ready, n)
                        nc.scalar.activation(f[:, :], proj_bank[0:H, 0:N], ACT.Copy).then_inc(f_copied, 1)
                    if j == 4 and F:
                        act.wait_ge(qk_ready, n)
                        at_least(act, q_stored, (n - 1) * 16 * 3)
                        at_least(act, k_stored, (n - 1) * 16 * 3)
                        nc.scalar.activation(q_parts[:, 0, :], q_ps, ACT.Copy, scale=SCALE)
                        nc.scalar.activation(k_parts[:, 0, :], k_ps, ACT.Copy).then_inc(qk_hi_done, 1)
                    if X:
                        exp(i - 1, s - 1, 2 * j)
                    if j == 2 and F:
                        act.wait_ge(xt_ready, n)
                        nc.scalar.activation(xt[:, :], proj_bank[:, 0:N], ACT.Copy).then_inc(xt_copied, 1)
                    if X:
                        exp(i - 1, s - 1, 2 * j + 1)
                    if j == 4 and X:
                        copy_out(i - 1, s - 1, 0)
                    if j == 2 and T:
                        copy_out(i - 2, s - 2, 1)
                    if j == 4 and F:
                        act.wait_ge(neg_abs_done, n)
                        nc.scalar.activation(exp_f[:, :], neg_abs[:, :], ACT.Exp).then_inc(exp_done, 1)
                        act.wait_ge(exp_done, n)
                        nc.scalar.activation(log_f[:, :], exp_f[:, :], ACT.Ln, bias=1.0).then_inc(log_done, 1)
                    if j == 4 and T:
                        act.wait_ge(attn_t_ready, i - 1)
                        nc.scalar.activation(attn_t[:, :], side_bank[:, 0:N], ACT.Copy).then_inc(attn_t_copied, 1)
            steps(act, step)

        @block.vector
        def _(dve):
            def tile(t):
                return x_all[:, bass.ds(t, 1), :].rearrange("p a d -> p (a d)")

            def row_max(i, s, p):
                dve.wait_ge(scores_ready, i * 12 + p + 1)
                t, first, heads = (0, 4 * p, 4) if p < 4 else (1, 2 * (p - 4), 2)
                nc.vector.tensor_reduce(neg_max[:, t, first:first + heads],
                                        score_bank[p % 2][:, :].rearrange("p (h n) -> p h n", h=heads),
                                        AX.X, ALU.max, negate=True).then_inc(max_done, 1)

            def low_max(i, s, t):
                dve.wait_ge(max_hi_done, i * 2 + t + 1)
                nc.vector.tensor_tensor(max_t[t][:, 1], side_bank[0:H, 0:P], max_t[t][:, 0].bitcast(FP32),
                                        ALU.subtract).then_inc(max_lo_done, 1)

            def normalise(i, s, t):
                dve.wait_ge(turned_ready, i * 2 + t + 1)
                out = out_bank[t][:, :].rearrange("p (n r) -> p n r", r=32)
                nc.vector.reciprocal(recip[:, t], out[:, :, HD]).then_inc(recip_done, 1)
                dve.wait_ge(recip_done, i * 2 + t + 1)
                nc.vector.tensor_tensor(attn[:, t].rearrange("p (g u) d -> p u g d", u=NU),
                                        out[:, :, 0:HD].rearrange("p (u g) d -> p u g d", u=NU),
                                        recip[:, t].rearrange("p (u g) -> p u g", u=NU).unsqueeze(3).broadcast_to([P, NU, NG, HD]),
                                        ALU.mult).then_inc(attn_done, 1)

            def step(i, s):
                S, X, T, F = 0 <= s < NSEQ, 0 <= s - 1 < NSEQ, 0 <= s - 2 < NSEQ, 0 <= s + 2 < NSEQ
                n = i + 3
                for j in range(6):
                    if S:
                        row_max(i, s, 2 * j)
                    if j == 0 and X:
                        low_max(i - 1, s - 1, 1)
                    if S:
                        row_max(i, s, 2 * j + 1)
                    if j == 0 and F:
                        for t in range(2):
                            last = nc.vector.bn_stats(stats[:, t], tile((i + 2) * 2 + t))
                        last.then_inc(stat_done, 1)
                        wait_apart(dve, stat_done, n, dve_waited)
                        for t in range(2):
                            last = nc.vector.bn_aggr(moments[:, t], stats[:, t])
                        last.then_inc(mom_done, 1)
                        dve.wait_ge(mom_done, n)
                        nc.vector.tensor_scalar(var_eps[:, :], moments[:, :, 1], EPS, None, ALU.add).then_inc(eps_done, 1)
                    if j == 1 and F:
                        dve.wait_ge(rstd_done, n)
                        for t in range(2):
                            last = nc.vector.tensor_scalar(xn[:, t], tile((i + 2) * 2 + t), moments[:, t, 0:1], rstd[:, t:t + 1],
                                                           ALU.subtract, ALU.mult)
                        last.then_inc(xn_done, 1)
                    if j == 3 and S:
                        low_max(i, s, 0)
                    if j == 3 and F:
                        dve.wait_ge(f_copied, n)
                        nc.vector.scalar_tensor_tensor(out=neg_abs[:, :], in0=f[:, :], scalar=-1.0, in1=f[:, :],
                                                       op0=ALU.mult, op1=ALU.min).then_inc(neg_abs_done, 1)
                    if j == 3 and T:
                        normalise(i - 2, s - 2, 1)
                    if j == 4 and F:
                        dve.wait_ge(qk_hi_done, n)
                        nc.vector.scalar_tensor_tensor(out=q_parts[:, 1, :], in0=q_ps, scalar=SCALE,
                                                       in1=q_parts[:, 0, :].bitcast(FP32), op0=ALU.mult, op1=ALU.subtract).then_inc(qk_lo_done, 1)
                        nc.vector.tensor_tensor(k_parts[:, 1, :], k_ps, k_parts[:, 0, :].bitcast(FP32),
                                                ALU.subtract).then_inc(qk_lo_done, 1)
                    if j == 5 and F:
                        dve.wait_ge(log_done, n)
                        nc.vector.scalar_tensor_tensor(out=log_sig[:, :], in0=f[:, :], scalar=0.0, in1=log_f[:, :],
                                                       op0=ALU.min, op1=ALU.subtract).then_inc(log_sig_done, 1)
                        dve.wait_ge(log_sig_done, n)
                        at_least(dve, c_lo_done, n - 1)
                        nc.vector.tensor_tensor_scan(neg_c[:, :], ones_row[:, :], log_sig[:, :], 0.0,
                                                     ALU.mult, ALU.subtract).then_inc(c_done, 1)
                    if j == 5 and X:
                        normalise(i - 1, s - 1, 0)
                    if j == 5 and T:
                        dve.wait_ge(proj_ready, i - 1)
                        pair = x_all[:, bass.ds((i - 2) * 2, 2), :].rearrange("p t d -> p (t d)")
                        nc.vector.tensor_tensor(pair, pair, side_bank[:, 0:2 * D], ALU.add).then_inc(proj_added, 1)
            steps(dve, step)

        @block.tensor
        def _(pe):
            pe.wait_ge(set_up, 2)
            pe.wait_ge(w_ordered, 2)
            pe.wait_ge(ones_in, 16 * 3 * (NG + 1))

            def scores(i, s, p):
                at_least(pe, max_done, i * 12 + p - 1)
                b, bank = s % 3, score_bank[p % 2]
                t, first, heads = (0, 4 * p, 4) if p < 4 else (1, 2 * (p - 4), 2)
                keys = (t + 1) * P
                for n in range(heads):
                    h = first + n
                    nc.tensor.matmul(bank[:, n * keys:(n + 1) * keys], q_rows[b][0:KR, h, t * P:(t + 1) * P],
                                     k_rows[b][0:KR, h % NU, 0:keys], start=n == 0, stop=False, skip_group_check=True)
                own = bank[:, :].rearrange("p (h n) -> p h n", h=heads)[:, :, keys - P:keys]
                nc.tensor.matmul(own, ident16[:, :], mask16[:, 0:heads, :], start=False, stop=True,
                                 skip_group_check=True).then_inc(scores_ready, 1)

            def turned_scores(i, s, n):
                if n == 0:
                    pe.wait_ge(max_in[0], (i + 1) * 32)
                if n == 4:
                    pe.wait_ge(max_in[1], (i + 1) * 32)
                at_least(pe, wt_exp, i * 12 + n - 1)
                b, bank = s % 3, wt_bank[n % 2]
                t, u, jt = (0, n, 0) if n < 4 else (1, (n - 4) // 2, n % 2)
                diagonal = jt == t
                last = nc.tensor.matmul(bank[:, :], k_rows[b][0:KM, u, jt * P:(jt + 1) * P],
                                        q_rows[b][0:KM, u:H:NU, t * P:(t + 1) * P], start=True, stop=not diagonal)
                if diagonal:
                    last = nc.tensor.matmul(bank[:, :], ident16[:, :], mask16_t[:, :, :], start=False, stop=True)
                last.then_inc(wt_ready, 1)

            def times_v(i, s, k):
                pe.wait_ge(wt_exp, i * 12 + 2 * k + 2)
                if k == 0:
                    at_least(pe, attn_done, i * 2 - 1)
                if k == 2:
                    at_least(pe, attn_done, i * 2)
                b, w = s % 3, weights[k % 3]
                for half in range(2):
                    for g in range(NG):
                        u, t, jt = (2 * k + half, 0, 0) if k < 2 else (k - 2, 1, half)
                        last = nc.tensor.matmul(out_bank[t][32 * g:32 * (g + 1), u * P:(u + 1) * P], v_sb[b][:, jt, NU * g + u, :],
                                                w[:, 4 * half + g, :], start=jt == 0, stop=jt == t)
                last.then_inc(av_done, 1)

            def turn_out(i, s, t):
                pe.wait_ge(out_copied, i * 2 + t + 1)
                for u in range(NU):
                    last = nc.tensor.transpose(out_bank[t][:, u * P:(u + 1) * P], out_t[:, t, u * P:(u + 1) * P], c["ident"][:, :])
                last.then_inc(turned_ready, 1)

            def turn_max(i, s, t):
                pe.wait_ge(max_done, i * 12 + (12 if t else 4))
                nc.tensor.transpose(side_bank[0:H, 0:P], neg_max[:, t],
                                    c["ident"][:, :]).then_inc(max_t_ready, 1)

            def step(i, s):
                S, X, T = 0 <= s < NSEQ, 0 <= s - 1 < NSEQ, 0 <= s - 2 < NSEQ
                V, F, n = 0 <= s + 1 < NSEQ, 0 <= s + 2 < NSEQ, i + 3
                for j in range(6):
                    if j == 0 and S:
                        pe.wait_ge(rows_in, (i + 1) * 16 * LOADS)
                    if S:
                        scores(i, s, 2 * j)
                        scores(i, s, 2 * j + 1)
                    if j == 0 and X:
                        pe.wait_ge(max_lo_done, (i - 1) * 2 + 1)
                        at_least(pe, proj_added, i - 2)
                        turn_max(i - 1, s - 1, 1)
                    if j == 1 and V:
                        if X:
                            pe.wait_ge(max_lo_done, i * 2)
                        else:
                            at_least(pe, v_copied, i + 1)
                        for t in range(2):
                            last = nc.tensor.matmul(side_bank[:, t * D:(t + 1) * D], xt[:, t * P:(t + 1) * P], c["Wv"][:, :],
                                                    start=True, stop=True)
                        last.then_inc(v_ready, 1)
                    if j == 2 and F:
                        at_least(pe, qk_lo_done, (n - 1) * 2)
                        pe.wait_ge(xn_done, n)
                        for t in range(2):
                            last = nc.tensor.transpose(proj_bank[:, t * P:(t + 1) * P], xn[:, t], c["ident"][:, :])
                        last.then_inc(xt_ready, 1)
                    if j == 3 and S:
                        if V:
                            pe.wait_ge(v_copied, i + 2)
                        else:
                            pe.wait_ge(max_lo_done, i * 2)
                        turn_max(i, s, 0)
                    if X:
                        turned_scores(i - 1, s - 1, 2 * j)
                        turned_scores(i - 1, s - 1, 2 * j + 1)
                    if j == 3 and T:
                        turn_out(i - 2, s - 2, 1)
                    if j == 5 and X:
                        turn_out(i - 1, s - 1, 0)
                    if j == 4 and T:
                        if S:
                            pe.wait_ge(max_lo_done, i * 2 + 1)
                        elif X:
                            pe.wait_ge(max_lo_done, i * 2)
                        else:
                            pe.wait_ge(proj_added, i - 2)
                        pe.wait_ge(attn_done, (i - 1) * 2)
                        for t in range(2):
                            last = nc.tensor.transpose(side_bank[:, t * P:(t + 1) * P],
                                                       attn[:, t].rearrange("p h d -> p (h d)"), c["ident"][:, :])
                        last.then_inc(attn_t_ready, 1)
                    if j < 2 and T:
                        times_v(i - 2, s - 2, j + 4)
                    if j >= 2 and X:
                        times_v(i - 1, s - 1, j - 2)
                    if j == 2 and F:
                        pe.wait_ge(xt_copied, n)
                        nc.tensor.matmul(proj_bank[0:H, 0:N], c["Wf"][:, :], xt[:, :], start=True, stop=True).then_inc(f_ready, 1)
                    if j == 3 and F:
                        pe.wait_ge(f_copied, n)
                        nc.tensor.matmul(q_ps, wq_gdu[:, :], xt[:, :], start=True, stop=True)
                        nc.tensor.matmul(k_ps, wk_gdu[:, :], xt[:, :], start=True, stop=True).then_inc(qk_ready, 1)
                    if j == 5 and T:
                        pe.wait_ge(attn_t_copied, i - 1)
                        for t in range(2):
                            last = nc.tensor.matmul(side_bank[:, t * D:(t + 1) * D], attn_t[:, t * P:(t + 1) * P], c["Wo"][:, :],
                                                    start=True, stop=True)
                        last.then_inc(proj_ready, 1)
            steps(pe, step)


def program(nc, x, Wq, Wk, Wv, Wo, Wf, Wg, We, be, out):
    B, N, D = x.shape
    H, E = Wf.shape[1], Wg.shape[1]
    T = B * N // P
    x_rows = x.rearrange("b n d -> (b n) d")
    out_rows = out.rearrange("b n d -> (b n) d")
    with ExitStack() as ctx:
        sb = lambda name, shape, dt: ctx.enter_context(nc.sbuf_tensor(name, shape, dt))
        banks = [ctx.enter_context(nc.psum_tensor(f"bank{i}", [P, BANK], FP32)) for i in range(8)]
        x_all = sb("x_all", [P, T, D], FP32)
        c = {
            "E": E, "H": H,
            "we": sb("we", [P, E, D], FP32), "wg": sb("wg", [P, E], FP32),
            "Wq": sb("wq", [P, D], FP32), "Wk": sb("wk", [P, D], FP32), "Wv": sb("wv", [P, D], FP32),
            "Wo": sb("wo", [P, D], FP32), "Wf": sb("wf", [P, H], FP32),
            "we_hi": sb("we_hi", [P, E * D], FP32R), "we_lo": sb("we_lo", [P, E * D], FP32R),
            "wg_hi": sb("wg_hi", [P, E], FP32R), "wg_lo": sb("wg_lo", [P, E], FP32R),
            "bias": sb("bias", [96, 4 * D], FP32), "bias_split": sb("bias_split", [96, 4 * D], FP32R),
            "ident": sb("ident", [P, P], FP32), "expert_no": sb("expert_no", [P, E], FP32),
            "minus_half": sb("minus_half", [P, 4], FP32),
        }
        w = {"Wq": Wq, "Wk": Wk, "Wv": Wv, "Wo": Wo, "Wf": Wf, "Wg": Wg, "We": We, "be": be}
        load_constants(nc, sb, w, c)
        moe_layer(nc, c, banks, x_all, "m1_", x_dram=x_rows)
        attention_layer(nc, c, banks, x_all, N)
        moe_layer(nc, c, banks, x_all, "m2_", out_dram=out_rows)


_INS = ["L0_attn_x", "L0_attn_Wq", "L0_attn_Wk", "L0_attn_Wv", "L0_attn_Wo", "L0_attn_Wf",
        "L0_ffn_Wg", "L0_ffn_We", "L0_ffn_be"]


def kernel(**inputs):
    import numpy as _np
    import concourse.bacc as _bacc
    from concourse import mybir as _mybir
    from concourse.bass_utils import run_bass_kernel_spmd as _run

    nc = _bacc.Bacc("TRN2", target_bir_lowering=False, num_devices=1)
    arrays, args = {}, []
    for name in _INS:
        a = _np.ascontiguousarray(inputs[name])
        arrays[f"in_{name}"] = a
        args.append(nc.dram_tensor(f"in_{name}", a.shape, _mybir.dt.from_np(a.dtype), kind="ExternalInput").ap())
    x = arrays["in_L0_attn_x"]
    args.append(nc.dram_tensor("out_x", x.shape, _mybir.dt.from_np(x.dtype), kind="ExternalOutput").ap())
    program(nc, *args)
    r = _run(nc, [arrays], core_ids=[0])
    return r.results[0]["out_x"]
```

```python
import concourse.bass as bass
from concourse import mybir
from contextlib import ExitStack

FP32 = mybir.dt.float32
FP32R = mybir.dt.float32r
BF16 = mybir.dt.bfloat16
U32 = mybir.dt.uint32
ALU = mybir.AluOpType
ACT = mybir.ActivationFunctionType
AX = mybir.AxisListType

P = 128
EPS = 1e-5
BANK = 512


def at_least(eng, sem, value):
    if isinstance(value, int) and value <= 0:
        return
    eng.wait_ge(sem, value)


def wait_apart(eng, sem, value, counted):
    eng.wait_ge(sem, value)
    eng.sem_inc(counted, 1)


def run_steps(eng, step, first, last, body, unroll, after=None):
    lo, hi = body
    for i in range(first, lo):
        step(i, i)
        if after is not None:
            after(i)
    with eng.Fori(0, (hi - lo) // unroll) as k:
        for part in range(unroll):
            step(k * unroll + (lo + part), lo + part)
    for i in range(hi, last):
        step(i, i)


def run_layers(eng, moe1, attention, moe2, groups, seqs, after=None):
    def moe_steps(part, first, last, after=None):
        run_steps(eng, lambda i, s: [part(i, s, k) for k in range(4)], first, last, (2, groups - 2), 2, after)

    def beside(order, i_attention, moe, i_moe):
        for at, which in enumerate(order):
            done = order[:at].count(which)
            if which == "a":
                attention(i_attention, i_attention, done)
            else:
                moe(i_moe, i_moe, done)

    moe_steps(moe1, -2, groups - 2, after)
    beside("amamammaaa", -2, moe1, groups - 2)
    beside("amamammaaa", -1, moe1, groups - 1)
    run_steps(eng, lambda i, s: [attention(i, s, k) for k in range(6)], 0, seqs - 1, (2, 2 + (seqs - 4) // 3 * 3), 3)
    beside("amaamamaam", seqs - 1, moe2, -2)
    beside("amaamamaam", seqs, moe2, -1)
    beside("aaaamamamm", seqs + 1, moe2, 0)
    moe_steps(moe2, 1, groups)


def constants(nc, ctx, w, c):
    sem = lambda name: ctx.enter_context(nc.semaphore(name))
    experts_in, small_in, bias_in = sem("experts_in"), sem("small_in"), sem("bias_in")
    filled, zeroed, split_hi, bias_hi = sem("filled"), sem("bias_zeroed"), sem("split_hi"), sem("bias_hi")
    pool_made, weights_split = sem("pool_made"), sem("weights_split")
    E, D = c["E"], P

    def load_weights(sp):
        sp.dma_start(c["we"][:, :, :], w["We"].rearrange("e h d -> h e d")).then_inc(experts_in, 16)
        sp.dma_start(c["wg"][:, :], w["Wg"]).then_inc(experts_in, 16)

    def load_rest(sp):
        sp.wait_ge(zeroed, 1)
        for part in range(3):
            for q in range(4):
                row = 32 * part + q * E
                sp.dma_start(c["bias"][row:row + E, q * D:(q + 1) * D], w["be"]).then_inc(bias_in, 16)
        for name in ("Wq", "Wk", "Wv", "Wo", "Wf"):
            sp.dma_start(c[name][:, :], w[name]).then_inc(small_in, 16)

    def make(pool):
        nc.gpsimd.memset(c["minus_half"][:, :], -0.5).then_inc(pool_made, 1)
        nc.gpsimd.memset(c["ident"][:, :], 0.0).then_inc(filled, 1)
        nc.gpsimd.memset(c["bias"][:, :], 0.0).then_inc(zeroed, 1)
        pool.wait_ge(filled, 1)
        nc.gpsimd.affine_select(out=c["ident"][:, :], in_=c["ident"][:, :], compare_op=ALU.not_equal, fill=1.0,
                                base=0, pattern=[[-1, P]], channel_multiplier=1).then_inc(filled, 1)
        nc.gpsimd.iota(c["expert_no"][:, :], pattern=[[1, E]], base=0, channel_multiplier=0,
                       allow_small_or_imprecise_dtypes=True).then_inc(pool_made, 1)
        pool.wait_ge(pool_made, 2)

    def split_high(act):
        nc.scalar.preload_act_table_set("natural_log_exp_and_others")
        act.wait_ge(experts_in, 16 * 2)
        nc.scalar.activation(c["we_hi"][:, :], c["we"][:, :, :].rearrange("p e d -> p (e d)"), ACT.Copy).then_inc(split_hi, 1)
        nc.scalar.activation(c["wg_hi"][:, :], c["wg"][:, :], ACT.Copy).then_inc(split_hi, 1)

    def split_low(dve):
        dve.wait_ge(split_hi, 2)
        nc.vector.tensor_tensor(c["wg_lo"][:, :], c["wg"][:, :], c["wg_hi"][:, :].bitcast(FP32), ALU.subtract)
        nc.vector.tensor_tensor(c["we_lo"][:, :], c["we"][:, :, :].rearrange("p e d -> p (e d)"),
                                c["we_hi"][:, :].bitcast(FP32), ALU.subtract).then_inc(weights_split, 1)
        dve.wait_ge(pool_made, 2)

    def split_bias(dve):
        dve.wait_ge(bias_in, 16 * 12)
        nc.vector.tensor_copy(c["bias_split"][:, :], c["bias"][:, :]).then_inc(bias_hi, 1)
        dve.wait_ge(bias_hi, 1)
        nc.vector.tensor_tensor(c["bias_split"][64:96, :], c["bias"][64:96, :],
                                c["bias_split"][64:96, :].bitcast(FP32), ALU.subtract).then_inc(bias_hi, 1)

    return dict(load_weights=load_weights, load_rest=load_rest, make=make, split_high=split_high,
                split_low=split_low, split_bias=split_bias, filled=filled, small_in=small_in,
                weights_split=weights_split, bias_hi=bias_hi)


def moe_tiles(nc, ctx, E, Q, D):
    sb = lambda name, shape, dt: ctx.enter_context(nc.sbuf_tensor("m_" + name, shape, dt))
    stats = sb("stats", [P, Q, 6], FP32)
    moments = sb("moments", [P, 2, Q, 2], FP32)
    var_eps = sb("var_eps", [P, 2, Q], FP32)
    rstd = sb("rstd", [P, 2, Q], FP32)
    neg_mean = sb("neg_mean", [P, 2, Q], FP32)
    shift = sb("shift", [P, 2, Q], FP32)
    xn = sb("xn", [P, Q, D], FP32)
    xt_hi = sb("xt_hi", [P, 2, Q * P], FP32R)
    xt_lo = sb("xt_lo", [P, 2, Q * P], FP32R)
    best = sb("best", [P, Q, 8], FP32)
    best_no = sb("best_no", [P, Q, 8], U32)
    gap = sb("gap", [P, Q], FP32)
    egap = sb("egap", [P, Q], FP32)
    denom = sb("denom", [P, Q], FP32)
    g12 = sb("g12", [P, 2, Q], FP32)
    hot = sb("hot", [P, 2, Q, E], FP32)
    gates = sb("gates", [P, 2, Q, E], FP32)
    gates3 = sb("gates3", [P, 3, Q * E], FP32R)
    gates_t = sb("gates_t", [3 * Q * E, P], FP32R)
    scaled = sb("scaled", [P, 2, 4, D], FP32)
    pair = sb("pair", [P, 2, 2, D], FP32)
    upper = sb("upper", [P, 2, D], FP32)
    lower = sb("lower", [P, 2, 4, D], FP32)
    return (stats, moments, var_eps, rstd, neg_mean, shift, xn, xt_hi, xt_lo,
            best, best_no, gap, egap, denom, g12, hot,
            gates, gates3, gates_t, scaled, pair, upper, lower)


def moe_layer(nc, ctx, c, made, tiles, banks, x_all, tag, x_dram=None, out_dram=None, before=None):
    E, Q, G = c["E"], 4, x_all.shape[1] // 4
    D = P
    sem = lambda name: ctx.enter_context(nc.semaphore(tag + name))
    (stats, moments, var_eps, rstd, neg_mean, shift, xn, xt_hi, xt_lo,
     best, best_no, gap, egap, denom, g12, hot,
     gates, gates3, gates_t, scaled, pair, upper, lower) = tiles

    y_low = [banks[0], banks[2]]
    y_high = [banks[1], banks[3]]
    gate_bank = banks[4]
    gates_t_view = gate_bank[0:3 * Q * E, P:2 * P]
    xt_bank = bias_bank = banks[5]
    logits = gate_bank[:, 0:Q * E].rearrange("p (q e) -> p q e", e=E)

    x_in = sem("x_in")
    stat_done, mom_done, eps_done = sem("stat_done"), sem("mom_done"), sem("eps_done")
    rstd_done, shift_done, xn_done = sem("rstd_done"), sem("shift_done"), sem("xn_done")
    xt_ready, hi_ready, lo_ready = sem("xt_ready"), sem("hi_ready"), sem("lo_ready")
    logits_ready, chain = sem("logits_ready"), sem("gate_chain")
    no_ready, egap_ready = sem("no_ready"), sem("egap_ready")
    gates_ready, gates_t_ready, gates_t_copied = sem("gates_ready"), sem("gates_t_ready"), sem("gates_t_copied")
    bias_ready, bias_added = sem("bias_ready"), sem("bias_added")
    y_ready, high_used = sem("y_ready"), sem("high_used")
    low_chain, pair_done, upper_done, upper_used = sem("low_chain"), sem("pair_done"), sem("upper_done"), sem("upper_used")
    stored, waited = sem("stored"), sem("waited")
    CH = 8

    def load_group(sp, g):
        at_least(sp, x_in, g * 16)
        sp.dma_start(x_all[:, bass.ds(g * Q, Q), :],
                     x_dram[bass.ds(g * (Q * P), Q * P), :].rearrange("(q p) d -> p q d", p=P)).then_inc(x_in, 16)

    def store(sp):
        with sp.Fori(0, G) as g:
            sp.wait_ge(upper_used, g * Q + Q)
            sp.dma_start(out_dram[bass.ds(g * (Q * P), Q * P), :].rearrange("(q p) d -> p q d", p=P),
                         x_all[:, bass.ds(g * Q, Q), :]).then_inc(stored, 16)
        sp.wait_ge(stored, 16 * G)

    def gpsimd(pool):
        def add_upper(i, q):
            t = i * Q + q
            pool.wait_ge(high_used, t + 1)
            nc.gpsimd.tensor_tensor(pair[:, q % 2], scaled[:, q % 2, 0:2], scaled[:, q % 2, 2:4],
                                    ALU.add).then_inc(pair_done, 1)
            pool.wait_ge(pair_done, t + 1)
            at_least(pool, upper_used, t - 1)
            nc.gpsimd.tensor_tensor(upper[:, q % 2], pair[:, q % 2, 0], pair[:, q % 2, 1],
                                    ALU.add).then_inc(upper_done, 1)

        def part(i, s, q):
            N, B, b, n = s + 2 < G, 0 <= s, s % 2, i + 3
            if B:
                add_upper(i, q)
            if q == 0 and N:
                pool.wait_ge(eps_done, n)
                nc.gpsimd.tensor_tensor(rstd[:, b], var_eps[:, b], c["minus_half"][:, 0:Q],
                                        ALU.pow).then_inc(rstd_done, 1)
                pool.wait_ge(rstd_done, n)
                nc.gpsimd.tensor_tensor(shift[:, b], neg_mean[:, b], rstd[:, b], ALU.mult).then_inc(shift_done, 1)
        return part

    def scalar(act):
        def experts(i, s, q):
            t = i * Q + q
            act.wait_ge(y_ready, t + 1)
            at_least(act, pair_done, t - 1)
            for j in range(4):
                last = nc.scalar.activation(scaled[:, q % 2, j], y_high[q % 2][:, j * D:(j + 1) * D], ACT.Copy,
                                            scale=gates[:, s % 2, q, 4 + j:5 + j])
            last.then_inc(high_used, 1)

        def part(i, s, q):
            b, n = s % 2, i + 3
            N, A, B = s + 2 < G, -1 <= s and s + 1 < G, 0 <= s
            if q == 0 and B:
                act.wait_ge(gates_t_ready, i + 1)
                nc.scalar.activation(gates_t[:, :], gates_t_view, ACT.Copy).then_inc(gates_t_copied, 1)
            if q == 3 and N:
                act.wait_ge(xt_ready, n)
                nc.scalar.activation(xt_hi[:, b], xt_bank[:, :], ACT.Copy).then_inc(hi_ready, 1)
            if B:
                experts(i, s, q)
            if q == 1 and A:
                act.wait_ge(chain, (i + 1) * CH + 2)
                nc.scalar.activation(egap[:, :], gap[:, :], ACT.Exp).then_inc(egap_ready, 1)
            if q == 1 and N:
                act.wait_ge(shift_done, n)
                for k in range(Q):
                    last = nc.scalar.activation(xn[:, k], x_all[:, bass.ds((i + 2) * Q + k, 1), :].rearrange("p a d -> p (a d)"),
                                                ACT.Identity, scale=rstd[:, b, k:k + 1], bias=shift[:, b, k:k + 1])
                last.then_inc(xn_done, 1)
        return part

    def vector(dve):
        tile = lambda t: x_all[:, bass.ds(t, 1), :].rearrange("p a d -> p (a d)")
        every = c["expert_no"][:, :].unsqueeze(1).unsqueeze(1).broadcast_to([P, 2, Q, E])

        def expert(i, s, q, j):
            t = i * Q + q
            if j == 0:
                dve.wait_ge(y_ready, t + 1)
            else:
                dve.wait_ge(low_chain, t * 4 + j)
            nc.vector.scalar_tensor_tensor(out=lower[:, q % 2, j], in0=y_low[q % 2][:, j * D:(j + 1) * D],
                                           scalar=gates[:, s % 2, q, j:j + 1],
                                           in1=tile(t) if j == 0 else lower[:, q % 2, j - 1],
                                           op0=ALU.mult, op1=ALU.add).then_inc(low_chain, 1)

        def finish(t, q):
            dve.wait_ge(upper_done, t + 1)
            dve.wait_ge(low_chain, t * 4 + 4)
            nc.vector.tensor_tensor(tile(t), lower[:, q % 2, 3], upper[:, q % 2], ALU.add).then_inc(upper_used, 1)

        def after_link(n, k):
            dve.wait_ge(chain, (n - 1) * CH + k)

        def part(i, s, q):
            N, A, B = s + 2 < G, -1 <= s and s + 1 < G, 0 <= s
            a, b, m, n = (s + 1) % 2, s % 2, i + 3, i + 2
            flat = gates[:, a].rearrange("p q e -> p (q e)")
            if q == 0 and N:
                if x_dram is not None:
                    dve.wait_ge(x_in, m * 16)
                else:
                    dve.wait_ge(before["x_done"], 2 * m)
                for k in range(Q):
                    last = nc.vector.bn_stats(stats[:, k], tile((i + 2) * Q + k))
                last.then_inc(stat_done, 1)
            if q == 0 and B:
                dve.wait_ge(bias_ready, i + 1)
                xg = x_all[:, bass.ds(i * Q, Q), :].rearrange("p q d -> p (q d)")
                nc.vector.tensor_tensor(xg, xg, bias_bank[:, :], ALU.add).then_inc(bias_added, 1)
            if q == 0 and N:
                wait_apart(dve, stat_done, m, waited)
                for k in range(Q):
                    last = nc.vector.bn_aggr(moments[:, b, k], stats[:, k])
                last.then_inc(mom_done, 1)
            if B:
                if q == 0:
                    dve.wait_ge(bias_added, i + 1)
                expert(i, s, q, 0)
            if q == 0 and N:
                dve.wait_ge(mom_done, m)
                nc.vector.tensor_scalar(neg_mean[:, b], moments[:, b, :, 0], -1.0, None, ALU.mult)
                nc.vector.tensor_scalar(var_eps[:, b], moments[:, b, :, 1], EPS, None, ALU.add).then_inc(eps_done, 1)
            if q == 1 and A:
                wait_apart(dve, logits_ready, n, waited)
                for k in range(Q):
                    last = nc.vector.max(best[:, k], logits[:, k])
                last.then_inc(chain, 1)
            if q == 2 and A:
                dve.wait_ge(no_ready, n)
                nc.vector.tensor_tensor(hot[:, :, :, :], every, best_no[:, :, 0:2].rearrange("p q r -> p r q").unsqueeze(3)
                                        .broadcast_to([P, 2, Q, E]), ALU.is_equal)
                dve.wait_ge(egap_ready, n)
                nc.vector.tensor_scalar(denom[:, :], egap[:, :], 2.0, 2.0, ALU.mult, ALU.add).then_inc(chain, 1)
            if q == 3 and A:
                after_link(n, 6)
                nc.vector.tensor_tensor(gates[:, a], hot[:, 0], hot[:, 1], ALU.add).then_inc(chain, 1)
            if B:
                expert(i, s, q, 1)
            if q == 1 and A:
                after_link(n, 1)
                nc.vector.tensor_tensor(gap[:, :], best[:, :, 1], best[:, :, 0], ALU.subtract).then_inc(chain, 1)
                for k in range(Q):
                    last = nc.vector.max_index(best_no[:, k], best[:, k], logits[:, k])
                last.then_inc(no_ready, 1)
            if q == 2 and A:
                after_link(n, 3)
                nc.vector.reciprocal(g12[:, 0], denom[:, :]).then_inc(chain, 1)
            if q == 3 and A:
                after_link(n, 7)
                nc.vector.tensor_copy(gates3[:, 0:3:2], flat.unsqueeze(1).broadcast_to([P, 2, Q * E])).then_inc(chain, 1)
            if B:
                expert(i, s, q, 2)
            if q == 3 and A:
                after_link(n, 8)
                nc.vector.tensor_tensor(gates3[:, 1], flat, gates3[:, 0].bitcast(FP32), ALU.subtract).then_inc(gates_ready, 1)
            if q == 3 and N:
                dve.wait_ge(hi_ready, m)
                nc.vector.tensor_tensor(xt_lo[:, b], xt_bank[:, :], xt_hi[:, b].bitcast(FP32), ALU.subtract).then_inc(lo_ready, 1)
            if B and not (s == 0 and q == 0):
                finish(i * Q + q - 1, (q - 1) % 2)
            if q == 2 and A:
                after_link(n, 4)
                nc.vector.tensor_tensor(g12[:, 1], egap[:, :], g12[:, 0], ALU.mult).then_inc(chain, 1)
            if B:
                expert(i, s, q, 3)
            if q == 2 and A:
                after_link(n, 5)
                nc.vector.tensor_tensor(hot[:, :, :, :], hot[:, :, :, :],
                                        g12[:, :, :].unsqueeze(3).broadcast_to([P, 2, Q, E]), ALU.mult).then_inc(chain, 1)
            if q == 3 and s == G - 1:
                finish(G * Q - 1, 1)
        return part

    def tensor(pe):
        def experts(i, s, q):
            t = i * Q + q
            b = s % 2
            at_least(pe, low_chain, (t - 1) * 4)
            at_least(pe, high_used, t - 1)
            hi, lo = xt_hi[:, b, q * P:(q + 1) * P], xt_lo[:, b, q * P:(q + 1) * P]
            H = 4 * D
            for k, (x_part, w_part) in enumerate(((hi, c["we_hi"]), (hi, c["we_lo"]), (lo, c["we_hi"]))):
                nc.tensor.matmul(y_low[q % 2][:, :], x_part, w_part[:, 0:H], start=k == 0, stop=k == 2)
                last = nc.tensor.matmul(y_high[q % 2][:, :], x_part, w_part[:, H:2 * H], start=k == 0, stop=k == 2)
            last.then_inc(y_ready, 1)

        def part(i, s, q):
            a, n = (s + 1) % 2, i + 2
            N, A, B = s + 2 < G, -1 <= s and s + 1 < G, 0 <= s
            if s == -1 and q == 0 and x_dram is not None:
                pe.wait_ge(made["weights_split"], 1)
            if s == -2 and q == 3 and x_dram is not None:
                pe.wait_ge(made["filled"], 2)
            if s == 0 and q == 0 and x_dram is None:
                pe.wait_ge(before["attn_done"], 4 * G - 1)
                pe.wait_ge(before["wt_exp"], 2 * G * 12)
            if B:
                experts(i, s, q)
            if q == 0 and B:
                pe.wait_ge(gates_ready, i + 1)
                nc.tensor.transpose(gates_t_view, gates3[:, :, :].rearrange("p k n -> p (k n)").bitcast(FP32),
                                    c["ident"][:, :]).then_inc(gates_t_ready, 1)
                pe.wait_ge(gates_t_copied, i + 1)
                if A:
                    pe.wait_ge(lo_ready, n)
                if s == 0 and x_dram is not None:
                    pe.wait_ge(made["bias_hi"], 2)
                nc.tensor.matmul(bias_bank[:, :], gates_t[:, :], c["bias_split"][:, :],
                                 start=True, stop=True).then_inc(bias_ready, 1)
            if q == 1 and A:
                pe.wait_ge(lo_ready, n)
                for k in range(Q):
                    hi, lo = xt_hi[:, a, k * P:(k + 1) * P], xt_lo[:, a, k * P:(k + 1) * P]
                    nc.tensor.matmul(logits[:, k], hi, c["wg_hi"][:, :], start=True, stop=False)
                    nc.tensor.matmul(logits[:, k], hi, c["wg_lo"][:, :], start=False, stop=False)
                    last = nc.tensor.matmul(logits[:, k], lo, c["wg_hi"][:, :], start=False, stop=True)
                last.then_inc(logits_ready, 1)
            if q == 3 and N:
                pe.wait_ge(xn_done, i + 3)
                if B:
                    pe.wait_ge(bias_added, i + 1)
                else:
                    at_least(pe, lo_ready, n)
                for k in range(Q):
                    last = nc.tensor.transpose(xt_bank[:, k * P:(k + 1) * P], xn[:, k], c["ident"][:, :])
                last.then_inc(xt_ready, 1)
        return part

    return dict(load_group=load_group, store=store, gpsimd=gpsimd, scalar=scalar, vector=vector, tensor=tensor,
                tiles_done=upper_used, high_used=high_used)


def attention_layer(nc, ctx, c, made, banks, x_all, S_LEN, before):
    H, D = c["H"], P
    NSEQ = x_all.shape[1] // 2
    HD = D // H
    NG, NU = 4, H // 4
    ROWS = 3 * HD + 2
    KR = NG * ROWS
    KM = KR + 2
    SCALE = float(HD) ** -0.5
    N = S_LEN
    sb = lambda name, shape, dt: ctx.enter_context(nc.sbuf_tensor("a_" + name, shape, dt))
    sem = lambda name: ctx.enter_context(nc.semaphore("a_" + name))
    stats = sb("stats", [P, 2, 6], FP32)
    moments = sb("moments", [P, 2, 2], FP32)
    var_eps = sb("var_eps", [P, 2], FP32)
    rstd = sb("rstd", [P, 2], FP32)
    xn = sb("xn", [P, 2, D], FP32)
    xt = sb("xt", [P, N], FP32)
    f = sb("f", [H, N], FP32)
    neg_abs = sb("neg_abs", [H, N], FP32)
    exp_f = sb("exp_f", [H, N], FP32)
    log_f = sb("log_f", [H, N], FP32)
    log_sig = sb("log_sig", [H, N], FP32)
    neg_c = sb("neg_c", [H, N], FP32)
    c_parts = sb("c_parts", [H, 2, N], FP32R)
    wq_gdu = sb("wq_gdu", [P, D], FP32)
    wk_gdu = sb("wk_gdu", [P, D], FP32)
    ones_row = sb("ones_row", [H, N], FP32)
    zero_row = sb("zero_row", [H, N], FP32)
    ones_r = sb("ones_r", [2, NU * N], FP32R)
    q_parts = sb("q_parts", [P, 2, N], FP32R)
    k_parts = sb("k_parts", [P, 2, N], FP32R)
    q_rows = [sb(f"q_rows{b}", [KM, H, N], FP32R) for b in range(3)]
    k_rows = [sb(f"k_rows{b}", [KM, NU, N], FP32R) for b in range(3)]
    v_sb = [sb(f"v{b}", [P, 2, H, 32], FP32) for b in range(3)]
    neg_max = sb("neg_max", [P, 2, H], FP32)
    max_t = [sb(f"max_t{t}", [H, 2, P], FP32R) for t in range(2)]
    weights = [sb(f"weights{n}", [P, 8, P], FP32) for n in range(3)]
    out_t = sb("out_t", [P, 2, NU * P], FP32)
    recip = sb("recip", [P, 2, H], FP32)
    attn = sb("attn", [P, 2, H, HD], FP32)
    attn_t = sb("attn_t", [P, N], FP32)
    ident16 = sb("ident16", [P, P], BF16)
    mask16 = sb("mask16", [P, 4, P], BF16)
    mask16_t = sb("mask16_t", [P, 4, P], BF16)

    score_bank = banks[0:2]
    wt_bank = banks[2:4]
    out_bank = banks[4:6]
    side_bank = banks[6]
    proj_bank = banks[7]
    q_ps, k_ps = proj_bank[:, 0:N], proj_bank[:, N:2 * N]

    set_up, zeroed, ones_in = sem("set_up"), sem("zeroed"), sem("ones_in")
    stat_done, mom_done, eps_done = sem("stat_done"), sem("mom_done"), sem("eps_done")
    rstd_done, xn_done = sem("rstd_done"), sem("xn_done")
    xt_ready, xt_copied = sem("xt_ready"), sem("xt_copied")
    f_ready, f_copied, neg_abs_done = sem("f_ready"), sem("f_copied"), sem("neg_abs_done")
    exp_done, log_done, log_sig_done = sem("exp_done"), sem("log_done"), sem("log_sig_done")
    c_done, c_hi_done, c_lo_done = sem("c_done"), sem("c_hi_done"), sem("c_lo_done")
    qk_ready, qk_hi_done, qk_lo_done = sem("qk_ready"), sem("qk_hi_done"), sem("qk_lo_done")
    v_ready, v_copied = sem("v_ready"), sem("v_copied")
    rows_in = sem("rows_in")
    scores_ready, max_done = sem("scores_ready"), sem("max_done")
    max_t_ready, max_hi_done, max_lo_done = sem("max_t_ready"), sem("max_hi_done"), sem("max_lo_done")
    max_in = [sem("max_in0"), sem("max_in1")]
    wt_ready, wt_exp, av_done = sem("wt_ready"), sem("wt_exp"), sem("av_done")
    out_copied, turned_ready = sem("out_copied"), sem("turned_ready")
    recip_done, attn_done = sem("recip_done"), sem("attn_done")
    attn_t_ready, attn_t_copied = sem("attn_t_ready"), sem("attn_t_copied")
    proj_ready, proj_added = sem("proj_ready"), sem("proj_added")
    dve_waited, sp_waited = sem("dve_waited"), sem("sp_waited")
    k_stored, q_stored, c_stored, w_ordered = sem("k_stored"), sem("q_stored"), sem("c_stored"), sem("w_ordered")
    LOADS = NG + 1
    raw = lambda tile: tile[(slice(None),) * len(tile.shape)].bitcast(FP32)
    q_dram = nc.dram_tensor("q_stage", (3, NG, 3 * HD, NU, N), FP32, kind="Internal").ap()
    k_dram = nc.dram_tensor("k_stage", (3, NG, ROWS, NU, N), FP32, kind="Internal").ap()

    f_part = lambda s: 2 if s >= 0 else 3

    def constant_rows(sp):
        sp.wait_ge(zeroed, 4)
        ones = ones_r[:, :].bitcast(FP32).rearrange("r (u n) -> r u n", u=NU)
        for b in range(3):
            for g in range(NG):
                sp.dma_start(raw(q_rows[b])[ROWS * g + 3 * HD:ROWS * (g + 1), NU * g:NU * (g + 1), :], ones).then_inc(ones_in, 16)
            sp.dma_start(raw(k_rows[b])[KR:KM, :, :], ones).then_inc(ones_in, 16)

    def sync(sp):
        def max_rows(i, s, t):
            for part, parts_done in enumerate((max_hi_done, max_lo_done)):
                sp.wait_ge(parts_done, i * 2 + t + 1)
                sp.dma_start(raw(q_rows[s % 3])[KR + part:KR + part + 1, :, t * P:(t + 1) * P],
                             raw(max_t[t])[:, part, :]).then_inc(max_in[t], 16)

        def step(i, s):
            if 0 <= s - 1 < NSEQ:
                max_rows(i - 1, s - 1, 1)
            if 0 <= s + 1 < NSEQ:
                b, n = (s + 1) % 3, i + 2
                if 0 <= s:
                    wait_apart(sp, scores_ready, i * 12 + 1, sp_waited)
                at_least(sp, wt_ready, (i - 1) * 12)
                sp.wait_ge(q_stored, n * 16 * 3)
                for g in range(NG):
                    sp.dma_start(raw(q_rows[b])[ROWS * g:ROWS * g + 3 * HD, NU * g:NU * (g + 1), :],
                                 q_dram[b, g]).then_inc(rows_in, 16)
                wait_apart(sp, k_stored, n * 16 * 3, sp_waited)
                sp.wait_ge(c_stored, n * 16 * 2)
                sp.dma_start(raw(k_rows[b])[0:KR, :, :], k_dram[b].rearrange("g r u n -> (g r) u n")).then_inc(rows_in, 16)
            if 0 <= s < NSEQ:
                max_rows(i, s, 0)
            if 0 <= s + 2 < NSEQ:
                b, n = (s + 2) % 3, i + 3
                sp.wait_ge(qk_lo_done, n * 2)
                for r, part in enumerate((0, 1, 0)):
                    sp.dma_start(k_dram[b, :, r * HD:(r + 1) * HD].rearrange("g d u n -> g (d u) n"),
                                 raw(k_parts)[:, part, :]).then_inc(k_stored, 16)
                for r, part in enumerate((0, 0, 1)):
                    sp.dma_start(q_dram[b, :, r * HD:(r + 1) * HD].rearrange("g d u n -> g (d u) n"),
                                 raw(q_parts)[:, part, :]).then_inc(q_stored, 16)
                sp.wait_ge(c_lo_done, n)
                for part in range(2):
                    sp.dma_start(k_dram[b, :, 3 * HD + part], raw(c_parts)[:, part, :]).then_inc(c_stored, 16)
        run_steps(sp, step, -2, NSEQ + 2, (2, 2 + (NSEQ - 4) // 3 * 3), 3)

    def set_up_rows(pool, b):
        nc.gpsimd.memset(q_rows[b][:, :, :].bitcast(U32), 0).then_inc(zeroed, 1)

    def set_up_columns(pool):
        for b in range(3):
            nc.gpsimd.memset(v_sb[b][:, :, :, HD + 1:], 0.0)
            nc.gpsimd.memset(v_sb[b][:, :, :, HD:HD + 1], 1.0)

    def set_up_masks(pool):
        nc.gpsimd.memset(ones_r[:, :].bitcast(FP32), 1.0).then_inc(zeroed, 1)
        nc.gpsimd.memset(ones_row[:, :], 1.0)
        nc.gpsimd.memset(zero_row[:, :], 0.0)
        nc.gpsimd.memset(ident16[:, :], 0.0)
        nc.gpsimd.memset(mask16_t[:, :, :], 0.0)
        nc.gpsimd.memset(mask16[:, :, :], 0.0).then_inc(set_up, 1)
        pool.wait_ge(set_up, 1)
        nc.gpsimd.affine_select(out=ident16[:, :], in_=ident16[:, :], compare_op=ALU.not_equal, fill=1.0,
                                base=0, pattern=[[-1, P]], channel_multiplier=1)
        nc.gpsimd.affine_select(out=mask16_t[:, :, :], in_=mask16_t[:, :, :], compare_op=ALU.is_ge, fill=-1e30,
                                base=0, pattern=[[0, 4], [1, P]], channel_multiplier=-1)
        nc.gpsimd.affine_select(out=mask16[:, :, :], in_=mask16[:, :, :], compare_op=ALU.is_ge, fill=-1e30,
                                base=0, pattern=[[0, 4], [-1, P]], channel_multiplier=1).then_inc(set_up, 1)
        pool.wait_ge(set_up, 2)

    def gpsimd(pool):
        def part(i, s, j):
            if j == 0 and 0 <= s + 2 < NSEQ:
                n = i + 3
                pool.wait_ge(eps_done, n)
                nc.gpsimd.tensor_tensor(rstd[:, :], var_eps[:, :], c["minus_half"][:, 0:2], ALU.pow).then_inc(rstd_done, 1)
            if j == 5 and 0 <= s + 2 < NSEQ:
                n = i + 3
                pool.wait_ge(c_done, n)
                at_least(pool, c_stored, (n - 1) * 16 * 2)
                nc.gpsimd.tensor_tensor(c_parts[:, 0], neg_c[:, :], zero_row[:, :], ALU.add).then_inc(c_hi_done, 1)
                pool.wait_ge(c_hi_done, n)
                nc.gpsimd.tensor_tensor(c_parts[:, 1], neg_c[:, :], c_parts[:, 0].bitcast(FP32), ALU.subtract).then_inc(c_lo_done, 1)
        return part

    def order_columns(act):
        act.wait_ge(made["small_in"], 16 * 5)
        for ordered, name in ((wq_gdu, "Wq"), (wk_gdu, "Wk")):
            nc.scalar.activation(ordered[:, :].rearrange("p (g d u) -> p g d u", g=NG, u=NU),
                                 c[name][:, :].rearrange("p (g u d) -> p g d u", g=NG, u=NU), ACT.Copy).then_inc(w_ordered, 1)

    def scalar(act):
        def copy_max(i, s, t):
            act.wait_ge(max_t_ready, i * 2 + t + 1)
            at_least(act, max_in[t], i * 32)
            nc.scalar.activation(max_t[t][:, 0], side_bank[0:H, 0:P], ACT.Copy).then_inc(max_hi_done, 1)

        def exp(i, s, n):
            act.wait_ge(wt_ready, i * 12 + n + 1)
            if n % 2 == 0:
                at_least(act, av_done, i * 6 + n // 2 - 2)
            half = 4 * (n % 2)
            nc.scalar.activation(weights[n // 2 % 3][:, half:half + 4, :].rearrange("p h n -> p (h n)"),
                                 wt_bank[n % 2][:, :], ACT.Exp).then_inc(wt_exp, 1)

        def copy_out(i, s, t):
            act.wait_ge(av_done, i * 6 + (6 if t else 2))
            nc.scalar.activation(out_t[:, t], out_bank[t][:, :], ACT.Copy).then_inc(out_copied, 1)

        def part(i, s, j):
            S, X, T = 0 <= s < NSEQ, 0 <= s - 1 < NSEQ, 0 <= s - 2 < NSEQ
            V, F, n = 0 <= s + 1 < NSEQ, 0 <= s + 2 < NSEQ, i + 3
            if j == 0 and X:
                copy_max(i - 1, s - 1, 1)
            if j == 2 and V:
                act.wait_ge(v_ready, i + 2)
                at_least(act, av_done, (i - 1) * 6)
                nc.scalar.activation(v_sb[(s + 1) % 3][:, :, :, 0:HD].rearrange("p t h d -> p (t h) d"),
                                     side_bank[:, 0:2 * D].rearrange("p (n d) -> p n d", d=HD), ACT.Copy).then_inc(v_copied, 1)
            if j == 3 and S:
                copy_max(i, s, 0)
            if j == f_part(s) + 1 and F:
                act.wait_ge(f_ready, n)
                nc.scalar.activation(f[:, :], proj_bank[0:H, 0:N], ACT.Copy).then_inc(f_copied, 1)
            if j == f_part(s) + 2 and F:
                act.wait_ge(qk_ready, n)
                at_least(act, q_stored, (n - 1) * 16 * 3)
                at_least(act, k_stored, (n - 1) * 16 * 3)
                nc.scalar.activation(q_parts[:, 0, :], q_ps, ACT.Copy, scale=SCALE)
                nc.scalar.activation(k_parts[:, 0, :], k_ps, ACT.Copy).then_inc(qk_hi_done, 1)
            if X:
                exp(i - 1, s - 1, 2 * j)
            if j == 2 and F:
                act.wait_ge(xt_ready, n)
                nc.scalar.activation(xt[:, :], proj_bank[:, 0:N], ACT.Copy).then_inc(xt_copied, 1)
            if X:
                exp(i - 1, s - 1, 2 * j + 1)
            if j == 4 and X:
                copy_out(i - 1, s - 1, 0)
            if j == 2 and T:
                copy_out(i - 2, s - 2, 1)
            if j == f_part(s) + 2 and F:
                act.wait_ge(neg_abs_done, n)
                nc.scalar.activation(exp_f[:, :], neg_abs[:, :], ACT.Exp).then_inc(exp_done, 1)
                act.wait_ge(exp_done, n)
                nc.scalar.activation(log_f[:, :], exp_f[:, :], ACT.Ln, bias=1.0).then_inc(log_done, 1)
            if j == 4 and T:
                act.wait_ge(attn_t_ready, i - 1)
                nc.scalar.activation(attn_t[:, :], side_bank[:, 0:N], ACT.Copy).then_inc(attn_t_copied, 1)
        return part

    def vector(dve):
        def tile(t):
            return x_all[:, bass.ds(t, 1), :].rearrange("p a d -> p (a d)")

        def row_max(i, s, p):
            dve.wait_ge(scores_ready, i * 12 + p + 1)
            t, first, heads = (0, 4 * p, 4) if p < 4 else (1, 2 * (p - 4), 2)
            nc.vector.tensor_reduce(neg_max[:, t, first:first + heads],
                                    score_bank[p % 2][:, :].rearrange("p (h n) -> p h n", h=heads),
                                    AX.X, ALU.max, negate=True).then_inc(max_done, 1)

        def low_max(i, s, t):
            dve.wait_ge(max_hi_done, i * 2 + t + 1)
            nc.vector.tensor_tensor(max_t[t][:, 1], side_bank[0:H, 0:P], max_t[t][:, 0].bitcast(FP32),
                                    ALU.subtract).then_inc(max_lo_done, 1)

        def normalise(i, s, t):
            dve.wait_ge(turned_ready, i * 2 + t + 1)
            out = out_bank[t][:, :].rearrange("p (n r) -> p n r", r=32)
            nc.vector.reciprocal(recip[:, t], out[:, :, HD]).then_inc(recip_done, 1)
            dve.wait_ge(recip_done, i * 2 + t + 1)
            nc.vector.tensor_tensor(attn[:, t].rearrange("p (g u) d -> p u g d", u=NU),
                                    out[:, :, 0:HD].rearrange("p (u g) d -> p u g d", u=NU),
                                    recip[:, t].rearrange("p (u g) -> p u g", u=NU).unsqueeze(3).broadcast_to([P, NU, NG, HD]),
                                    ALU.mult).then_inc(attn_done, 1)

        def part(i, s, j):
            S, X, T, F = 0 <= s < NSEQ, 0 <= s - 1 < NSEQ, 0 <= s - 2 < NSEQ, 0 <= s + 2 < NSEQ
            n = i + 3
            if S:
                row_max(i, s, 2 * j)
            if j == 0 and X:
                low_max(i - 1, s - 1, 1)
            if S:
                row_max(i, s, 2 * j + 1)
            if j == 0 and F:
                if s <= 0:
                    dve.wait_ge(before["tiles_done"], 2 * (s + 3) if s < 0 else 2 * NSEQ)
                for t in range(2):
                    last = nc.vector.bn_stats(stats[:, t], tile((i + 2) * 2 + t))
                last.then_inc(stat_done, 1)
                wait_apart(dve, stat_done, n, dve_waited)
                for t in range(2):
                    last = nc.vector.bn_aggr(moments[:, t], stats[:, t])
                last.then_inc(mom_done, 1)
                dve.wait_ge(mom_done, n)
                nc.vector.tensor_scalar(var_eps[:, :], moments[:, :, 1], EPS, None, ALU.add).then_inc(eps_done, 1)
            if j == 1 and F:
                dve.wait_ge(rstd_done, n)
                for t in range(2):
                    last = nc.vector.tensor_scalar(xn[:, t], tile((i + 2) * 2 + t), moments[:, t, 0:1], rstd[:, t:t + 1],
                                                   ALU.subtract, ALU.mult)
                last.then_inc(xn_done, 1)
            if j == 3 and S:
                low_max(i, s, 0)
            if j == f_part(s) + 1 and F:
                dve.wait_ge(f_copied, n)
                nc.vector.scalar_tensor_tensor(out=neg_abs[:, :], in0=f[:, :], scalar=-1.0, in1=f[:, :],
                                               op0=ALU.mult, op1=ALU.min).then_inc(neg_abs_done, 1)
            if j == 3 and T:
                normalise(i - 2, s - 2, 1)
            if j == f_part(s) + 2 and F:
                dve.wait_ge(qk_hi_done, n)
                nc.vector.scalar_tensor_tensor(out=q_parts[:, 1, :], in0=q_ps, scalar=SCALE,
                                               in1=q_parts[:, 0, :].bitcast(FP32), op0=ALU.mult, op1=ALU.subtract).then_inc(qk_lo_done, 1)
                nc.vector.tensor_tensor(k_parts[:, 1, :], k_ps, k_parts[:, 0, :].bitcast(FP32),
                                        ALU.subtract).then_inc(qk_lo_done, 1)
            if j == 5 and F:
                dve.wait_ge(log_done, n)
                nc.vector.scalar_tensor_tensor(out=log_sig[:, :], in0=f[:, :], scalar=0.0, in1=log_f[:, :],
                                               op0=ALU.min, op1=ALU.subtract).then_inc(log_sig_done, 1)
                dve.wait_ge(log_sig_done, n)
                at_least(dve, c_lo_done, n - 1)
                nc.vector.tensor_tensor_scan(neg_c[:, :], ones_row[:, :], log_sig[:, :], 0.0,
                                             ALU.mult, ALU.subtract).then_inc(c_done, 1)
            if j == 5 and X:
                normalise(i - 1, s - 1, 0)
            if j == 5 and T:
                dve.wait_ge(proj_ready, i - 1)
                pair = x_all[:, bass.ds((i - 2) * 2, 2), :].rearrange("p t d -> p (t d)")
                nc.vector.tensor_tensor(pair, pair, side_bank[:, 0:2 * D], ALU.add).then_inc(proj_added, 1)
        return part

    def tensor(pe):
        def scores(i, s, p):
            at_least(pe, max_done, i * 12 + p - 1)
            b, bank = s % 3, score_bank[p % 2]
            t, first, heads = (0, 4 * p, 4) if p < 4 else (1, 2 * (p - 4), 2)
            keys = (t + 1) * P
            for n in range(heads):
                h = first + n
                nc.tensor.matmul(bank[:, n * keys:(n + 1) * keys], q_rows[b][0:KR, h, t * P:(t + 1) * P],
                                 k_rows[b][0:KR, h % NU, 0:keys], start=n == 0, stop=False, skip_group_check=True)
            own = bank[:, :].rearrange("p (h n) -> p h n", h=heads)[:, :, keys - P:keys]
            nc.tensor.matmul(own, ident16[:, :], mask16[:, 0:heads, :], start=False, stop=True,
                             skip_group_check=True).then_inc(scores_ready, 1)

        def turned_scores(i, s, n):
            if n == 0:
                pe.wait_ge(max_in[0], (i + 1) * 32)
            if n == 4:
                pe.wait_ge(max_in[1], (i + 1) * 32)
            at_least(pe, wt_exp, i * 12 + n - 1)
            b, bank = s % 3, wt_bank[n % 2]
            t, u, jt = (0, n, 0) if n < 4 else (1, (n - 4) // 2, n % 2)
            diagonal = jt == t
            last = nc.tensor.matmul(bank[:, :], k_rows[b][0:KM, u, jt * P:(jt + 1) * P],
                                    q_rows[b][0:KM, u:H:NU, t * P:(t + 1) * P], start=True, stop=not diagonal)
            if diagonal:
                last = nc.tensor.matmul(bank[:, :], ident16[:, :], mask16_t[:, :, :], start=False, stop=True)
            last.then_inc(wt_ready, 1)

        def times_v(i, s, k):
            pe.wait_ge(wt_exp, i * 12 + 2 * k + 2)
            if k == 0:
                at_least(pe, attn_done, i * 2 - 1)
            if k == 2:
                at_least(pe, attn_done, i * 2)
            b, w = s % 3, weights[k % 3]
            for half in range(2):
                for g in range(NG):
                    u, t, jt = (2 * k + half, 0, 0) if k < 2 else (k - 2, 1, half)
                    last = nc.tensor.matmul(out_bank[t][32 * g:32 * (g + 1), u * P:(u + 1) * P], v_sb[b][:, jt, NU * g + u, :],
                                            w[:, 4 * half + g, :], start=jt == 0, stop=jt == t)
            last.then_inc(av_done, 1)

        def turn_out(i, s, t):
            pe.wait_ge(out_copied, i * 2 + t + 1)
            for u in range(NU):
                last = nc.tensor.transpose(out_bank[t][:, u * P:(u + 1) * P], out_t[:, t, u * P:(u + 1) * P], c["ident"][:, :])
            last.then_inc(turned_ready, 1)

        def turn_max(i, s, t):
            pe.wait_ge(max_done, i * 12 + (12 if t else 4))
            nc.tensor.transpose(side_bank[0:H, 0:P], neg_max[:, t],
                                c["ident"][:, :]).then_inc(max_t_ready, 1)

        def part(i, s, j):
            S, X, T = 0 <= s < NSEQ, 0 <= s - 1 < NSEQ, 0 <= s - 2 < NSEQ
            V, F, n = 0 <= s + 1 < NSEQ, 0 <= s + 2 < NSEQ, i + 3
            if s == -2 and j == 0:
                pe.wait_ge(w_ordered, 2)
            if s == 0 and j == 0:
                pe.wait_ge(set_up, 2)
                pe.wait_ge(ones_in, 16 * 3 * (NG + 1))
                pe.wait_ge(before["tiles_done"], 2 * NSEQ)
                pe.wait_ge(before["high_used"], 2 * NSEQ)
            if j == 0 and S:
                pe.wait_ge(rows_in, (i + 1) * 16 * LOADS)
            if S:
                scores(i, s, 2 * j)
                scores(i, s, 2 * j + 1)
            if j == 0 and X:
                pe.wait_ge(max_lo_done, (i - 1) * 2 + 1)
                at_least(pe, proj_added, i - 2)
                turn_max(i - 1, s - 1, 1)
            if j == 1 and V:
                if X:
                    pe.wait_ge(max_lo_done, i * 2)
                else:
                    at_least(pe, v_copied, i + 1)
                for t in range(2):
                    last = nc.tensor.matmul(side_bank[:, t * D:(t + 1) * D], xt[:, t * P:(t + 1) * P], c["Wv"][:, :],
                                            start=True, stop=True)
                last.then_inc(v_ready, 1)
            if j == 2 and F:
                at_least(pe, qk_lo_done, (n - 1) * 2)
                pe.wait_ge(xn_done, n)
                for t in range(2):
                    last = nc.tensor.transpose(proj_bank[:, t * P:(t + 1) * P], xn[:, t], c["ident"][:, :])
                last.then_inc(xt_ready, 1)
            if j == 3 and S:
                if V:
                    pe.wait_ge(v_copied, i + 2)
                else:
                    pe.wait_ge(max_lo_done, i * 2)
                turn_max(i, s, 0)
            if X:
                turned_scores(i - 1, s - 1, 2 * j)
                turned_scores(i - 1, s - 1, 2 * j + 1)
            if j == 3 and T:
                turn_out(i - 2, s - 2, 1)
            if j == 5 and X:
                turn_out(i - 1, s - 1, 0)
            if j == 4 and T:
                if S:
                    pe.wait_ge(max_lo_done, i * 2 + 1)
                elif X:
                    pe.wait_ge(max_lo_done, i * 2)
                else:
                    pe.wait_ge(proj_added, i - 2)
                pe.wait_ge(attn_done, (i - 1) * 2)
                for t in range(2):
                    last = nc.tensor.transpose(side_bank[:, t * P:(t + 1) * P],
                                               attn[:, t].rearrange("p h d -> p (h d)"), c["ident"][:, :])
                last.then_inc(attn_t_ready, 1)
            if j < 2 and T:
                times_v(i - 2, s - 2, j + 4)
            if j >= 2 and X:
                times_v(i - 1, s - 1, j - 2)
            if j == f_part(s) and F:
                pe.wait_ge(xt_copied, n)
                nc.tensor.matmul(proj_bank[0:H, 0:N], c["Wf"][:, :], xt[:, :], start=True, stop=True).then_inc(f_ready, 1)
            if j == f_part(s) + 1 and F:
                pe.wait_ge(f_copied, n)
                nc.tensor.matmul(q_ps, wq_gdu[:, :], xt[:, :], start=True, stop=True)
                nc.tensor.matmul(k_ps, wk_gdu[:, :], xt[:, :], start=True, stop=True).then_inc(qk_ready, 1)
            if j == 5 and T:
                pe.wait_ge(attn_t_copied, i - 1)
                for t in range(2):
                    last = nc.tensor.matmul(side_bank[:, t * D:(t + 1) * D], attn_t[:, t * P:(t + 1) * P], c["Wo"][:, :],
                                            start=True, stop=True)
                last.then_inc(proj_ready, 1)
        return part

    return dict(constant_rows=constant_rows, sync=sync, set_up_rows=set_up_rows, set_up_columns=set_up_columns, set_up_masks=set_up_masks,
                order_columns=order_columns, gpsimd=gpsimd, scalar=scalar, vector=vector, tensor=tensor,
                x_done=proj_added, attn_done=attn_done, wt_exp=wt_exp)


def program(nc, x, Wq, Wk, Wv, Wo, Wf, Wg, We, be, out):
    B, N, D = x.shape
    H, E = Wf.shape[1], Wg.shape[1]
    T = B * N // P
    x_rows = x.rearrange("b n d -> (b n) d")
    out_rows = out.rearrange("b n d -> (b n) d")
    with ExitStack() as ctx:
        sb = lambda name, shape, dt: ctx.enter_context(nc.sbuf_tensor(name, shape, dt))
        banks = [ctx.enter_context(nc.psum_tensor(f"bank{i}", [P, BANK], FP32)) for i in range(8)]
        x_all = sb("x_all", [P, T, D], FP32)
        c = {
            "E": E, "H": H,
            "we": sb("we", [P, E, D], FP32), "wg": sb("wg", [P, E], FP32),
            "Wq": sb("wq", [P, D], FP32), "Wk": sb("wk", [P, D], FP32), "Wv": sb("wv", [P, D], FP32),
            "Wo": sb("wo", [P, D], FP32), "Wf": sb("wf", [P, H], FP32),
            "we_hi": sb("we_hi", [P, E * D], FP32R), "we_lo": sb("we_lo", [P, E * D], FP32R),
            "wg_hi": sb("wg_hi", [P, E], FP32R), "wg_lo": sb("wg_lo", [P, E], FP32R),
            "bias": sb("bias", [96, 4 * D], FP32), "bias_split": sb("bias_split", [96, 4 * D], FP32R),
            "ident": sb("ident", [P, P], FP32), "expert_no": sb("expert_no", [P, E], FP32),
            "minus_half": sb("minus_half", [P, 4], FP32),
        }
        w = {"Wq": Wq, "Wk": Wk, "Wv": Wv, "Wo": Wo, "Wf": Wf, "Wg": Wg, "We": We, "be": be}
        made = constants(nc, ctx, w, c)
        Q, G = 4, T // 4
        tiles = moe_tiles(nc, ctx, E, Q, D)
        moe1 = moe_layer(nc, ctx, c, made, tiles, banks, x_all, "m1_", x_dram=x_rows)
        attention = attention_layer(nc, ctx, c, made, banks, x_all, N, before=moe1)
        moe2 = moe_layer(nc, ctx, c, made, tiles, banks[1:5] + [banks[0], banks[7]], x_all, "m2_",
                         out_dram=out_rows, before=attention)
        block = ctx.enter_context(nc.Block())

        @block.sync
        def _(sp):
            moe1["load_group"](sp, 0)
            made["load_weights"](sp)
            moe1["load_group"](sp, 1)
            made["load_rest"](sp)
            with sp.Fori(2, G) as g:
                moe1["load_group"](sp, g)
            attention["constant_rows"](sp)
            attention["sync"](sp)
            moe2["store"](sp)

        @block.gpsimd
        def _(pool):
            made["make"](pool)

            attention["set_up_rows"](pool, 0)

            def after(i):
                if i == -2:
                    attention["set_up_rows"](pool, 1)
                    attention["set_up_columns"](pool)
                if i == -1:
                    attention["set_up_rows"](pool, 2)
                    attention["set_up_masks"](pool)
            run_layers(pool, moe1["gpsimd"](pool), attention["gpsimd"](pool), moe2["gpsimd"](pool), G, B, after)

        @block.scalar
        def _(act):
            made["split_high"](act)

            def after(i):
                if i == -1:
                    attention["order_columns"](act)
            run_layers(act, moe1["scalar"](act), attention["scalar"](act), moe2["scalar"](act), G, B, after)

        @block.vector
        def _(dve):
            def after(i):
                if i == -2:
                    made["split_low"](dve)
                    made["split_bias"](dve)
            run_layers(dve, moe1["vector"](dve), attention["vector"](dve), moe2["vector"](dve), G, B, after)

        @block.tensor
        def _(pe):
            run_layers(pe, moe1["tensor"](pe), attention["tensor"](pe), moe2["tensor"](pe), G, B)


_INS = ["L0_attn_x", "L0_attn_Wq", "L0_attn_Wk", "L0_attn_Wv", "L0_attn_Wo", "L0_attn_Wf",
        "L0_ffn_Wg", "L0_ffn_We", "L0_ffn_be"]


def kernel(**inputs):
    import numpy as _np
    import concourse.bacc as _bacc
    from concourse import mybir as _mybir
    from concourse.bass_utils import run_bass_kernel_spmd as _run

    nc = _bacc.Bacc("TRN2", target_bir_lowering=False, num_devices=1)
    arrays, args = {}, []
    for name in _INS:
        a = _np.ascontiguousarray(inputs[name])
        arrays[f"in_{name}"] = a
        args.append(nc.dram_tensor(f"in_{name}", a.shape, _mybir.dt.from_np(a.dtype), kind="ExternalInput").ap())
    x = arrays["in_L0_attn_x"]
    args.append(nc.dram_tensor("out_x", x.shape, _mybir.dt.from_np(x.dtype), kind="ExternalOutput").ap())
    program(nc, *args)
    r = _run(nc, [arrays], core_ids=[0])
    return r.results[0]["out_x"]
```
